# Optimizing a Trainium2 kernel written in Bass

```python
import numpy as np
import jax
import jax.numpy as jnp

def _softmax(x, axis=-1):
    return jax.nn.softmax(x, axis=axis)

def _gelu(x):
    return jax.nn.gelu(x, approximate=True)

def _silu(x):
    return jax.nn.silu(x)

def _sigmoid(x):
    return jax.nn.sigmoid(x)

def _layernorm(x, axis=-1, eps=1e-05):
    m = jnp.mean(x, axis=axis, keepdims=True)
    v = jnp.var(x, axis=axis, keepdims=True)
    return (x - m) / jnp.sqrt(v + eps)

def _scatter_add(tgt, idx, src, axis=0):
    return tgt.at[idx].add(src)

def _segment_sum(src, seg, n):
    return jax.ops.segment_sum(src, seg, n)
kernel_name = 'mk_adj_resnorm_d2_adj_r2_12004c'

def setup_inputs(seed: int=0):
    np.random.seed(seed)
    _w = jnp.asarray

    def _rec_inputs():
        import jax
        import jax.numpy as jnp
        _gk = jax.random.key(seed)
        x = -8.776e-05 + 1 * jax.random.normal(jax.random.fold_in(_gk, 1), (10000, 128), jnp.float32)
        _w = (1.0 + jnp.arange(10000, dtype=jnp.float32)) ** (-0.5)
        _w = _w / _w.mean()
        _pij = jnp.clip(0.0004 * _w[:, None] * _w[None, :], 0.0, 1.0)
        _a = jax.random.uniform(jax.random.fold_in(_gk, 2), (10000, 10000)) < _pij
        _a = jnp.logical_or(_a, jnp.eye(10000, dtype=bool))
        _af = _a.astype(jnp.float32)
        _af = _af * jax.random.uniform(jax.random.fold_in(_gk, 3), (10000, 10000), jnp.float32, 0.05, 1)
        adj = _af
        return (x, adj)
    x, adj = _rec_inputs()

    def _L0_gnn_setup():
        import jax, jax.numpy as jnp
        import numpy as np
        N_USER = 10000
        N_ITEM = 10000
        HID = 128
        key = jax.random.key(seed)
        k1, k2, k3, k4, k5, k6, k7 = jax.random.split(key, 7)
        scale = 1.0 / np.sqrt(HID)
        return {'user_feat': jax.random.normal(k1, (N_USER, HID), dtype=jnp.float32), 'item_feat': jax.random.normal(k2, (N_ITEM, HID), dtype=jnp.float32), 'adj': jax.random.uniform(k3, (N_USER, N_ITEM), dtype=jnp.float32), 'W_item': jax.random.uniform(k4, (HID, HID), dtype=jnp.float32, minval=-scale, maxval=scale), 'b_item': jax.random.uniform(k5, (HID,), dtype=jnp.float32, minval=-scale, maxval=scale), 'W_user': jax.random.uniform(k6, (HID, HID), dtype=jnp.float32, minval=-scale, maxval=scale), 'b_user': jax.random.uniform(k7, (HID,), dtype=jnp.float32, minval=-scale, maxval=scale)}
    _L0_gnn_all = _L0_gnn_setup()
    _L0_gnn_in = {k: v for k, v in _L0_gnn_all.items() if k in ('item_feat', 'W_item', 'b_item', 'W_user', 'b_user')}
    del _L0_gnn_all

    def _L1_gnn_setup():
        import jax, jax.numpy as jnp
        import numpy as np
        N = 4096
        IN_DIM = 128
        OUT_DIM = 128
        ALPHA = 0.2
        NEG_INF = -9000000000000000.0
        key = jax.random.key(seed)
        k_h, k_w, k_a, k_adj = jax.random.split(key, 4)
        h = jax.random.normal(k_h, (N, IN_DIM), dtype=jnp.float32)
        w_bound = float(np.sqrt(6.0 / (IN_DIM + OUT_DIM)))
        W = jax.random.uniform(k_w, (IN_DIM, OUT_DIM), dtype=jnp.float32, minval=-w_bound, maxval=w_bound)
        a_bound = float(np.sqrt(6.0 / (2 * OUT_DIM + 1)))
        a = jax.random.uniform(k_a, (2 * OUT_DIM, 1), dtype=jnp.float32, minval=-a_bound, maxval=a_bound)
        adj = (jax.random.uniform(k_adj, (N, N), dtype=jnp.float32) < 0.01).astype(jnp.float32)
        adj = jnp.maximum(adj, jnp.eye(N, dtype=jnp.float32))
        return {'h': h, 'adj': adj, 'W': W, 'a': a}
    _L1_gnn_all = _L1_gnn_setup()
    _L1_gnn_in = {k: v for k, v in _L1_gnn_all.items() if k in ('W', 'a')}
    del _L1_gnn_all
    return {'x': x, 'adj': adj, 'L0_gnn_item_feat': _L0_gnn_in['item_feat'], 'L0_gnn_W_item': _L0_gnn_in['W_item'], 'L0_gnn_b_item': _L0_gnn_in['b_item'], 'L0_gnn_W_user': _L0_gnn_in['W_user'], 'L0_gnn_b_user': _L0_gnn_in['b_user'], 'L1_gnn_W': _L1_gnn_in['W'], 'L1_gnn_a': _L1_gnn_in['a']}

def reference(x, adj, L0_gnn_item_feat, L0_gnn_W_item, L0_gnn_b_item, L0_gnn_W_user, L0_gnn_b_user, L1_gnn_W, L1_gnn_a):
    import jax
    import jax.numpy as jnp

    def _L0_gnn_ref(user_feat, item_feat, adj, W_item, b_item, W_user, b_user):
        import jax, jax.numpy as jnp
        import numpy as np
        N_USER = 10000
        N_ITEM = 10000
        HID = 128
        h = item_feat @ W_item.T + b_item
        b = user_feat @ W_user.T + b_user
        return jax.nn.relu(adj @ h + b)

    def _L1_gnn_ref(h, adj, W, a):
        import jax, jax.numpy as jnp
        import numpy as np
        N = 4096
        IN_DIM = 128
        OUT_DIM = 128
        ALPHA = 0.2
        NEG_INF = -9000000000000000.0
        Wh = h @ W
        Wh1 = Wh @ a[:OUT_DIM, :]
        Wh2 = Wh @ a[OUT_DIM:, :]
        e = jax.nn.leaky_relu(Wh1 + Wh2.T, negative_slope=ALPHA)
        attention = jax.nn.softmax(jnp.where(adj > 0, e, NEG_INF), axis=1)
        h_prime = attention @ Wh
        return jax.nn.elu(h_prime)
    x = _layernorm(x + _L0_gnn_ref(x, L0_gnn_item_feat, adj, L0_gnn_W_item, L0_gnn_b_item, L0_gnn_W_user, L0_gnn_b_user), axis=-1)
    x = _layernorm(x + _L1_gnn_ref(x, adj, L1_gnn_W, L1_gnn_a), axis=-1)
    return x

_drawn_inputs = setup_inputs


def setup_inputs(seed=0):
    import zlib

    import numpy as np

    out = dict(_drawn_inputs(seed))
    spreads = {}
    factors = {}
    for name, (base, spread) in spreads.items():
        noise = np.random.default_rng([zlib.crc32(name.encode()), seed]).standard_normal(out[name].shape)
        drawn = base * np.exp(spread * noise) if base else spread * noise
        out[name] = jnp.asarray(drawn.astype(out[name].dtype))
    for name, factor in factors.items():
        out[name] = (out[name] * factor).astype(out[name].dtype)
    return out
```

```python
from contextlib import ExitStack

import concourse.bass as bass
from concourse import mybir

ALU = mybir.AluOpType
ACT = mybir.ActivationFunctionType
F32 = mybir.dt.float32
U8 = mybir.dt.uint8
AX_X = mybir.AxisListType.X

P = 128
D = 128
Q = 32
A = P // Q
IB = 512
TPB = IB // P
GPB = IB // Q
JC = 1024
JA = JC // A
SPC = JA // Q
HG = GPB // 2
LN_EPS = 1e-5
SLOPE = 0.2
A_SHIFT = 40.0
C_SHIFT = -72.0
F_CAP = 30.0


def resnorm_two_graph_layers(nc, x, adj, item, w_item, b_item, w_user, b_user, w_att, a_att, out):
    N = x.shape[0]
    NB = N // IB
    TAIL = N - NB * IB
    TG = -(-TAIL // Q)
    TW = TG * Q
    NC = N // JC + 1
    LJ = (N - (NC - 1) * JC) // A
    LS = -(-LJ // Q)
    LPAD = LS * Q - LJ
    STEPS = (NC - 1) * SPC + LS
    NP = NB * IB + IB
    RAW = 5 if (2 * NC) % 5 == 0 else 4
    LOFF = JA - LJ
    RAWW = JA + LPAD
    UNROLL = 6
    GROUPS = (STEPS - 1) // UNROLL
    DEN = D + 1
    WHG = -(-STEPS // 3)
    THIRDS = [0, STEPS // 3, 2 * (STEPS // 3), STEPS]
    assert N % A == 0 and 0 < TAIL < IB and 0 <= LPAD < Q and 0 < LJ <= JA and NC % 2 == 0 and NC >= 4
    assert (2 * NC) % RAW == 0 and GROUPS * UNROLL + 1 == STEPS and NB % 2 == 1 and TG > HG
    assert SPC * D == 2 * IB

    def steps_of(c):
        return SPC if c < NC - 1 else LS

    def cols_of(c):
        return JA if c < NC - 1 else LJ

    with ExitStack() as ctx:
        def sb(name, shape, dt=F32):
            return ctx.enter_context(nc.sbuf_tensor(name, shape, dt))

        def sem(name):
            return ctx.enter_context(nc.semaphore(name))

        mask_dram = nc.dram_tensor("mask_scratch", [NB + 1, P, STEPS * IB], U8, kind="Internal").ap()
        x1_dram = nc.dram_tensor("x1_scratch", [NP, D], F32, kind="Internal").ap()
        s_dram = nc.dram_tensor("s_scratch", [1, NP], F32, kind="Internal").ap()

        area_h = sb("area_h", [P, STEPS * DEN])
        h = area_h[:, 0:STEPS * D].rearrange("p (s d) -> p s d", d=D)
        awh = area_h[:, :].rearrange("p (s d) -> p s d", d=DEN)
        raw_words = RAW * HG * RAWW
        t_words = 2 * SPC * IB
        area_1 = sb("area_1", [P, max(raw_words + t_words, NP + STEPS * IB // 4)])
        raw = area_1[:, 0:raw_words].rearrange("p (r g w) -> p r g w", r=RAW, g=HG)
        adj_t = area_1[:, raw_words:raw_words + t_words].rearrange("p (b w) -> p b w", b=2)
        f_row = area_1[:, 0:NP]
        mask_even = area_1[:, NP:NP + STEPS * IB // 4].bitcast(U8)
        area_x = sb("area_x", [P, max(NP, STEPS * IB // 4, 5 * JC)])
        x1_t = area_x[:, 0:NP]
        mask_odd = area_x[:, 0:STEPS * IB // 4].bitcast(U8)
        item_t = area_x[:, 0:2 * JC].rearrange("p (b w) -> p b w", b=2)
        item_in = area_x[:, 2 * JC:4 * JC].rearrange("p (b t d) -> p b t d", b=2, d=D)
        item_plain = area_x[:, 4 * JC:5 * JC]
        masks = [mask_even, mask_odd]

        area_m = sb("area_m", [P, 2, SPC * IB // 4])
        mask_out = area_m.bitcast(U8)
        x1_steps = area_m
        ident = sb("ident", [P, P])
        ones = sb("ones", [P, P])
        inv_d = sb("inv_d", [P, P])
        w_in = sb("w_in", [P, 3, D])
        w_t = sb("w_t", [P, 3, D])
        a_cols = sb("a_cols", [P, 2])
        w_den = sb("w_den", [P, DEN])
        w_ts = sb("w_ts", [P, 2])
        b_item_row = sb("b_item_row", [P, D])
        b_user_col = sb("b_user_col", [P, 1])
        eps_col = sb("eps_col", [P, 1])
        area_s = sb("area_s", [P, UNROLL + 1, IB])
        x_in = area_s[:, 0, :].rearrange("p (t d) -> p t d", d=D)
        x_t, yz, zc, sq, x1_blk = (area_s[:, i, :] for i in range(1, 6))
        x1_rows = area_s[:, 6, :].rearrange("p (t d) -> p t d", d=D)
        prob = area_s
        ts_row = sb("ts_row", [2, IB])
        t_max = sb("t_max", [2, NB + 1])
        t_top = sb("t_top", [1, 1])
        shift = sb("shift", [P, 4])
        a_col = sb("a_col", [P, STEPS])
        c_col = sb("c_col", [P, STEPS])
        x_sums = sb("x_sums", [P, NB + 1])
        x_sum = sb("x_sum", [P, 1])
        x_mean = sb("x_mean", [P, P])
        wh_mean = sb("wh_mean", [P, D])
        o_sb = sb("o_sb", [P, TPB, DEN])
        den = sb("den", [P, 3, TPB])
        el = sb("el", [P, 3, IB])
        x1_in = sb("x1_in", [P, TPB, D])
        stats = sb("stats", [P, TPB, 6])
        mv = sb("mv", [P, TPB, 2])
        std_o = sb("std_o", [P, TPB])
        rstd_o = sb("rstd_o", [P, TPB])
        o_out = sb("o_out", [P, TPB, D])

        banks = [ctx.enter_context(nc.psum_tensor(f"bank{i}", [P, IB], F32)) for i in range(8)]
        acc, ps_x, ps_mean, ps_var, ps_rows, ps_ts = banks[0:6]

        s_wload = sem("s_wload")
        s_const = sem("s_const")
        s_wt = sem("s_wt")
        s_wt_sb = sem("s_wt_sb")
        s_wa = sem("s_wa")
        s_wa_sb = sem("s_wa_sb")
        s_item = [sem("s_item0"), sem("s_item1")]
        s_item_ps = sem("s_item_ps")
        s_item_t = sem("s_item_t")
        s_h_ps = sem("s_h_ps")
        s_h = sem("s_h")
        s_pad = sem("s_pad")
        s_raw = [sem(f"s_raw{i}") for i in range(RAW)]
        s_half = sem("s_half")
        s_used = sem("s_used")
        s_mask = sem("s_mask")
        s_stored = [sem("s_stored0"), sem("s_stored1")]
        s_xin = sem("s_xin")
        s_xps = sem("s_xps")
        s_xt = sem("s_xt")
        s_y = sem("s_y")
        s_z = sem("s_z")
        s_mean = sem("s_mean")
        s_zc = sem("s_zc")
        s_sq = sem("s_sq")
        s_var = sem("s_var")
        s_std = sem("s_std")
        s_rstd = sem("s_rstd")
        s_x1 = sem("s_x1")
        s_x1t = sem("s_x1t")
        s_x1p = sem("s_x1p")
        s_x1r = sem("s_x1r")
        s_tsr = sem("s_tsr")
        s_tmax = sem("s_tmax")
        s_x1d = sem("s_x1d")
        s_sd = sem("s_sd")
        s_top = sem("s_top")
        s_topb = sem("s_topb")
        s_shift = sem("s_shift")
        s_perm = sem("s_perm")
        s_item_p = sem("s_item_p")
        s_wh = sem("s_wh")
        s_ac = sem("s_ac")
        s_awh = sem("s_awh")
        s_sload = [sem("s_sload0"), sem("s_sload1")]
        s_m0 = [sem(f"s_m0{i}") for i in range(3)]
        s_fcap = sem("s_fcap")
        s_f = sem("s_f")
        s_xs = sem("s_xs")
        s_xm = sem("s_xm")
        s_whm = sem("s_whm")
        s_wm = sem("s_wm")
        s_mld = [sem("s_mld0"), sem("s_mld1")]
        s_p = sem("s_p")
        s_pu = sem("s_pu")
        s_ev = sem("s_ev")
        s_den = sem("s_den")
        s_num = sem("s_num")
        s_h2 = sem("s_h2")
        s_exp = sem("s_exp")
        s_el = sem("s_el")
        s_x1i = sem("s_x1i")
        s_zz = sem("s_zz")
        s_st = sem("s_st")
        s_mv = sem("s_mv")
        s_rs = sem("s_rs")
        s_rr = sem("s_rr")
        s_fin = sem("s_fin")
        s_out = sem("s_out")

        block = ctx.enter_context(nc.Block())

        def layer1_blocks(eng, body):
            body(0, IB, True)
            body(1, IB, False)
            with eng.Fori(2, NB) as k:
                body(k, IB, False)
            body(NB, TW, False)

        def layer2_blocks(eng, body):
            body(0, 0, IB, True)
            body(1, 1, IB, False)
            body(2, 0, IB, False)
            with eng.Fori(3, NB - 1, 2) as k:
                body(k, 1, IB, False)
                body(k + 1, 0, IB, False)
            body(NB, 1, TW, False)

        def in_step_order(copy, dst, src, last_chunk):
            if not last_chunk:
                return [copy(dst.rearrange("p (s a j) -> p a s j", a=A, j=Q), src.rearrange("p (a s j) -> p a s j", a=A, j=Q))]
            whole = LJ // Q
            one = copy(dst[:, 0:whole * P].rearrange("p (s a j) -> p a s j", a=A, j=Q),
                       src[:, 0:A * LJ].rearrange("p (a w) -> p a w", a=A)[:, :, 0:whole * Q].rearrange("p a (s j) -> p a s j", j=Q))
            two = copy(dst[:, whole * P:(whole + 1) * P].rearrange("p (a j) -> p a j", a=A),
                       src[:, whole * Q:whole * Q + A * LJ].rearrange("p (a w) -> p a w", a=A)[:, :, 0:Q])
            return [one, two]

        def tiles_of(width):
            return [(t, min(P, width - t * P)) for t in range(-(-width // P))]

        @block.sync
        def _(sp):
            for n, w in enumerate((w_item, w_user, w_att)):
                sp.dma_start(w_in[:, n, :], w).then_inc(s_wload, 16)
            sp.dma_start(a_cols[:, 0:1], a_att[0:D, :]).then_inc(s_wload, 16)
            sp.dma_start(a_cols[:, 1:2], a_att[D:2 * D, :]).then_inc(s_wload, 16)
            sp.dma_start(b_item_row[:, :], b_item.rearrange("(a d) -> a d", a=1).to_broadcast([P, D])).then_inc(s_wload, 16)
            sp.dma_start(b_user_col[:, :], b_user.rearrange("(d a) -> d a", a=1)).then_inc(s_wload, 16)

            def load_half(k, n, width):
                c, half = n // 2, n % 2
                slot = n % RAW
                groups = HG if half == 0 or width == IB else width // Q - HG
                rows = Q if half == 0 or width == IB else TAIL - HG * Q - (groups - 1) * Q
                off = 0 if c < NC - 1 else LOFF
                if not (isinstance(k, int) and k * 2 * NC + n < RAW):
                    sp.wait_ge(s_half, k * (2 * NC) + n - RAW + 1)
                for a in range(A):
                    cols = slice(c * JC + a * cols_of(c), c * JC + (a + 1) * cols_of(c))
                    if rows == Q:
                        src = adj[bass.ds(k * IB + half * HG * Q, groups * Q), cols].rearrange("(g i) w -> i g w", i=Q)
                        dst = raw[a * Q:(a + 1) * Q, slot, 0:groups, off:off + cols_of(c)]
                    else:
                        assert groups == 1
                        src = adj[N - rows:N, cols]
                        dst = raw[a * Q:a * Q + rows, slot, 0, off:off + cols_of(c)]
                    sp.dma_start(dst, src).then_inc(s_raw[slot], 16)

            def load_item(c):
                if c >= 2:
                    sp.wait_ge(s_item_ps, c - 1)
                lo, hi = c * JC, min(N, (c + 1) * JC)
                full = (hi - lo) // P
                sp.dma_start(item_in[:, c % 2, 0:full, :], item[lo:lo + full * P, :].rearrange("(t p) d -> p t d", p=P)).then_inc(s_item[c % 2], 16)
                if hi - lo > full * P:
                    sp.dma_start(item_in[0:hi - lo - full * P, c % 2, full, :], item[lo + full * P:hi, :]).then_inc(s_item[c % 2], 16)

            def load_x(k, width):
                if not (isinstance(k, int) and k == 0):
                    sp.wait_ge(s_xps, k)
                if width == IB:
                    rows = x[bass.ds(k * IB, IB), :].rearrange("(t p) d -> p t d", p=P)
                    for t in (0, TPB // 2):
                        sp.dma_start(x_in[:, t:t + TPB // 2, :], rows[:, t:t + TPB // 2, :]).then_inc(s_xin, 16)
                else:
                    full = TAIL // P
                    sp.dma_start(x_in[:, 0:full, :], x[NB * IB:NB * IB + full * P, :].rearrange("(t p) d -> p t d", p=P)).then_inc(s_xin, 16)
                    sp.dma_start(x_in[0:TAIL - full * P, full, :], x[NB * IB + full * P:N, :]).then_inc(s_xin, 16)

            def block_loads(k, width, first):
                for n in range(2 * NC):
                    if first and n < RAW:
                        continue
                    if n == 0:
                        load_x(k, width)
                    load_half(k, n, width)

            load_item(0)
            load_item(1)
            load_x(0, IB)
            for n in range(RAW):
                load_half(0, n, IB)
            for c in range(2, NC):
                load_item(c)
            layer1_blocks(sp, block_loads)

            def load_mask(k, par, width, signals):
                for i in range(3):
                    lo, hi = THIRDS[i] * width, THIRDS[i + 1] * width
                    sp.dma_start(masks[par][:, lo:hi],
                                 mask_dram[bass.ds(k, 1), :, lo:hi].rearrange("o p w -> (o p) w")).then_inc(signals[i], 16)

            def load_x1(k):
                if not (isinstance(k, int) and k == 0):
                    sp.wait_ge(s_zz, k)
                sp.dma_start(x1_in[:, :, :], x1_dram[bass.ds(k * IB, IB), :].rearrange("(t p) d -> p t d", p=P)).then_inc(s_x1i, 16)

            def next_mask(k, par, width):
                sp.wait_ge(s_p, k * STEPS)
                load_mask(k + 1, 1 - par, width, [s_mld[1 - par]] * 3)

            sp.wait_ge(s_half, 2 * NC * (NB + 1))
            sp.wait_ge(s_used, NC * (NB + 1))
            sp.wait_ge(s_mask, NC * (NB + 1))
            sp.wait_ge(s_stored[0], 8 * NC * (NB + 1))
            sp.wait_ge(s_stored[1], 8 * NC * (NB + 1))
            sp.wait_ge(s_sd, 16 * (NB + 1))
            sp.dma_start(f_row[:, 0:IB], s_dram[:, 0:IB].to_broadcast([P, IB])).then_inc(s_sload[0], 16)
            load_mask(0, 0, IB, s_m0)
            sp.dma_start(f_row[:, IB:NP], s_dram[:, IB:NP].to_broadcast([P, NP - IB])).then_inc(s_sload[1], 16)
            sp.wait_ge(s_x1d, 16 * (NB + 1))
            load_x1(0)
            sp.wait_ge(s_awh, WHG)
            load_mask(1, 1, IB, [s_mld[1]] * 3)
            next_mask(1, 1, IB)
            load_x1(1)
            next_mask(2, 0, IB)
            load_x1(2)
            with sp.Fori(3, NB - 3, 2) as k:
                next_mask(k, 1, IB)
                load_x1(k)
                next_mask(k + 1, 0, IB)
                load_x1(k + 1)
            next_mask(NB - 2, 1, IB)
            load_x1(NB - 2)
            next_mask(NB - 1, 0, TW)
            load_x1(NB - 1)
            load_x1(NB)

        @block.gpsimd
        def _(pool):
            nc.gpsimd.memset(ones[:, :], 1.0).then_inc(s_const, 1)
            nc.gpsimd.memset(ident[:, :], 0.0).then_inc(s_const, 1)
            pool.wait_ge(s_const, 2)
            nc.gpsimd.affine_select(out=ident[:, :], in_=ident[:, :], compare_op=ALU.not_equal, fill=1.0, base=0,
                                    pattern=[[-1, P]], channel_multiplier=1).then_inc(s_const, 1)
            nc.gpsimd.memset(inv_d[:, :], 1.0 / D).then_inc(s_const, 1)
            nc.gpsimd.memset(item_plain[:, :], 0.0).then_inc(s_const, 1)
            nc.gpsimd.memset(eps_col[:, :], LN_EPS).then_inc(s_const, 1)
            for n in (2 * NC - 2, 2 * NC - 1):
                nc.gpsimd.memset(raw[:, n % RAW, :, JA:RAWW], 0.0).then_inc(s_pad, 1)

            def keep_x1(k, width, first):
                pool.wait_ge(s_x1, k + 1)
                nc.gpsimd.tensor_copy(x1_t[:, bass.ds(k * IB, width)], x1_blk[:, 0:width]).then_inc(s_x1t, 1)

            layer1_blocks(pool, keep_x1)
            nc.gpsimd.memset(x1_t[:, NB * IB + TW:NB * IB + TW + Q], 0.0).then_inc(s_x1t, 1)

            F_PARTS = ((0, IB), (IB, NP))
            pool.wait_ge(s_shift, 1)
            for i, (lo, hi) in enumerate(F_PARTS):
                pool.wait_ge(s_sload[i], 16)
                nc.gpsimd.tensor_scalar(f_row[:, lo:hi], f_row[:, lo:hi], shift[:, 3:4], None, ALU.min).then_inc(s_fcap, 1)
            pool.wait_ge(s_xs, NB + 2)
            nc.gpsimd.tensor_scalar(x_mean[:, :], ones[:, :], x_sum[:, 0:1], 1.0 / N, ALU.mult, ALU.mult).then_inc(s_xm, 1)

            def epilogue(k, par, width, first):
                nt = len(tiles_of(width))
                w = nt * D
                num = o_sb[:, 0:nt, 0:D]
                e0, e1, e2 = (el[:, i, 0:w].rearrange("p (t d) -> p t d", d=D) for i in range(3))
                if first:
                    pool.wait_ge(s_wm, 1)
                pool.wait_ge(s_den, 3 * (k + 1))
                nc.gpsimd.tensor_tensor(e0, wh_mean[:, None, :].to_broadcast([P, nt, D]),
                                        den[:, 0, 0:nt, None].to_broadcast([P, nt, D]), ALU.mult).then_inc(s_num, 1)
                pool.wait_ge(s_num, 3 * k + 1)
                nc.gpsimd.tensor_tensor(e1, e0, num, ALU.add).then_inc(s_num, 1)
                pool.wait_ge(s_num, 3 * k + 2)
                nc.gpsimd.tensor_tensor(e0, e1, den[:, 2, 0:nt, None].to_broadcast([P, nt, D]), ALU.mult).then_inc(s_num, 1)
                pool.wait_ge(s_num, 3 * k + 3)
                nc.gpsimd.nop(nofuse=True)
                nc.gpsimd.tensor_scalar(el[:, 1, 0:w], el[:, 0, 0:w], 0.0, None, ALU.min).then_inc(s_h2, 1)
                if not (isinstance(k, int) and k == 0):
                    pool.wait_ge(s_fin, k)
                    nc.gpsimd.nop(nofuse=True)
                nc.gpsimd.tensor_scalar(el[:, 2, 0:w], el[:, 0, 0:w], 0.0, -1.0, ALU.max, ALU.add).then_inc(s_h2, 1)
                pool.wait_ge(s_exp, k + 1)
                pool.wait_ge(s_h2, 2 * k + 2)
                nc.gpsimd.tensor_tensor(el[:, 0, 0:w], el[:, 1, 0:w], el[:, 2, 0:w], ALU.add).then_inc(s_el, 1)
                pool.wait_ge(s_el, k + 1)
                pool.wait_ge(s_x1i, 16 * (k + 1))
                nc.gpsimd.tensor_tensor(e2, e0, x1_in[:, 0:nt, :], ALU.add).then_inc(s_zz, 1)

            layer2_blocks(pool, epilogue)

        @block.tensor
        def _(pe):
            pe.wait_ge(s_const, 4)
            pe.wait_ge(s_wload, 16 * 7)
            for n in range(3):
                mm = nc.tensor.transpose(banks[n][:, 0:D], w_in[:, n, :], ident[:, :])
            mm.then_inc(s_wt, 1)
            pe.wait_ge(s_wt_sb, 1)
            nc.tensor.matmul(banks[3][:, 0:1], w_t[:, 2, :], a_cols[:, 1:2], start=True, stop=True)
            nc.tensor.matmul(banks[3][:, 1:2], w_t[:, 2, :], a_cols[:, 0:1], start=True, stop=True).then_inc(s_wa, 1)

            def item_transposes(c):
                n = min(N, (c + 1) * JC) - c * JC
                pe.wait_ge(s_item[c % 2], 16 * (c // 2 + 1) if c < NC - 1 else 16 * (c // 2 + 2))
                if c >= 1:
                    pe.wait_ge(s_item_t, c)
                for t in range(-(-n // P)):
                    m = min(P, n - t * P)
                    mm = nc.tensor.transpose(banks[4 + t // 4][:, (t % 4) * P:(t % 4) * P + m],
                                             item_in[0:m, c % 2, t, :], ident[0:m, 0:m])
                mm.then_inc(s_item_ps, 1)

            def h_products(c):
                pe.wait_ge(s_item_t, c + 1)
                if c >= 1:
                    pe.wait_ge(s_h, c)
                for s in range(steps_of(c)):
                    mm = nc.tensor.matmul(banks[6 + s // 4][:, (s % 4) * D:(s % 4 + 1) * D],
                                          item_t[:, c % 2, s * P:(s + 1) * P], w_t[:, 0, :], start=True, stop=True)
                mm.then_inc(s_h_ps, 1)

            item_transposes(0)
            for c in range(NC):
                if c + 1 < NC:
                    item_transposes(c + 1)
                h_products(c)

            def norm_mean(k, width):
                pe.wait_ge(s_z, k + 1)
                nc.tensor.matmul(ps_mean[:, 0:width], inv_d[:, :], yz[:, 0:width], start=True, stop=True).then_inc(s_mean, 1)

            def norm_var(k, width):
                pe.wait_ge(s_sq, k + 1)
                nc.tensor.matmul(ps_var[:, 0:width], inv_d[:, :], sq[:, 0:width], start=True, stop=True).then_inc(s_var, 1)

            def x1_products(k, width):
                pe.wait_ge(s_x1, k + 1)
                if not (isinstance(k, int) and k == 0):
                    pe.wait_ge(s_x1r, k)
                    pe.wait_ge(s_tsr, k)
                for t, m in tiles_of(width):
                    nc.tensor.transpose(ps_rows[0:m, t * P:t * P + D], x1_blk[:, t * P:t * P + m], ident[:, :])
                nc.tensor.matmul(ps_ts[0:2, 0:width], w_ts[:, :], x1_blk[:, 0:width], start=True, stop=True).then_inc(s_x1p, 1)

            def contract(k, width, first):
                pe.wait_ge(s_xin, 32 * (k + 1))
                if not first:
                    pe.wait_ge(s_xt, k)
                live = tiles_of(width) if width == IB else tiles_of(TAIL)
                for t, m in live:
                    mm = nc.tensor.transpose(ps_x[:, t * P:t * P + m], x_in[0:m, t, :], ident[0:m, 0:m])
                mm.then_inc(s_xps, 1)
                for c in range(NC):
                    pe.wait_ge(s_half, k * (2 * NC) + 2 * c + 2)
                    if c == 0 and not first:
                        pe.wait_ge(s_y, k)
                    for s in range(steps_of(c)):
                        mm = nc.tensor.matmul(acc[:, 0:width], h[:, c * SPC + s, :],
                                              adj_t[:, c % 2, s * width:(s + 1) * width],
                                              start=(c == 0 and s == 0), stop=(c == NC - 1 and s == LS - 1))
                    mm.then_inc(s_used, 1)
                    if c == 0:
                        pe.wait_ge(s_xt, k + 1)
                        nc.tensor.matmul(acc[:, 0:width], w_t[:, 1, :], x_t[:, 0:width], start=False, stop=False)
                    if not first:
                        if c == 1:
                            norm_mean(k - 1, IB)
                        if c == 2:
                            norm_var(k - 1, IB)
                        if c == 3:
                            x1_products(k - 1, IB)

            pe.wait_ge(s_h, NC)
            layer1_blocks(pe, contract)
            norm_mean(NB, TW)
            norm_var(NB, TW)
            x1_products(NB, TW)

            pe.wait_ge(s_top, 1)
            nc.tensor.matmul(ps_mean[:, 0:1], ones[0:1, :], t_top[0:1, 0:1], start=True, stop=True).then_inc(s_topb, 1)

            def right_products(g):
                if g >= 4:
                    pe.wait_ge(s_awh, g - 3)
                for b in range(3 * g, min(STEPS, 3 * g + 3)):
                    c, s = b // SPC, b % SPC
                    pe.wait_ge(s_perm, c + 1)
                    mm = nc.tensor.matmul(banks[4 + g % 4][:, (b - 3 * g) * DEN:(b - 3 * g + 1) * DEN],
                                          x1_steps[:, c % 2, s * P:(s + 1) * P], w_den[:, :], start=True, stop=True)
                mm.then_inc(s_wh, 1)

            pe.wait_ge(s_x1t, NB + 2)
            pe.wait_ge(s_x1r, NB + 1)
            pe.wait_ge(s_tsr, NB + 1)
            for g in range(3):
                right_products(g)

            def weighted(par, width, right, slot, start, stop):
                for t, m in tiles_of(width):
                    bank = banks[2 * par + t // 2]
                    mm = nc.tensor.matmul(bank[0:m, (t % 2) * DEN:(t % 2 + 1) * DEN], prob[:, slot, t * P:t * P + m],
                                          right, start=start and t % 2 == 0, stop=stop, skip_group_check=True)
                mm.then_inc(s_pu, 1)

            def layer2(k, par, width, first):
                if not (isinstance(k, int) and k < 2):
                    pe.wait_ge(s_ev, 2 * (k - 1))
                pe.wait_ge(s_p, k * STEPS + 1)
                if first:
                    right_products(3)
                    pe.wait_ge(s_awh, 1)
                weighted(par, width, awh[:, 0, :], UNROLL, True, False)
                if first:
                    for b in range(1, STEPS):
                        if b % 3 == 0 and b // 3 + 3 < WHG:
                            right_products(b // 3 + 3)
                        pe.wait_ge(s_awh, b // 3 + 1)
                        pe.wait_ge(s_p, b + 1)
                        weighted(par, width, awh[:, b, :], (b - 1) % UNROLL, False, b == STEPS - 1)
                    pe.wait_ge(s_xm, 1)
                    nc.tensor.matmul(banks[4][:, 0:D], x_mean[:, :], w_in[:, 2, :], start=True, stop=True).then_inc(s_whm, 1)
                    return
                with pe.Fori(0, GROUPS - 1) as g:
                    for j in range(UNROLL):
                        pe.wait_ge(s_p, k * STEPS + g * UNROLL + j + 2)
                        weighted(par, width, area_h[:, bass.ds(g * (UNROLL * DEN) + (j + 1) * DEN, DEN)], j, False, False)
                for j in range(UNROLL):
                    b = (GROUPS - 1) * UNROLL + j + 1
                    pe.wait_ge(s_p, k * STEPS + b + 1)
                    weighted(par, width, awh[:, b, :], j, False, b == STEPS - 1)

            layer2_blocks(pe, layer2)

        @block.vector
        def _(dve):
            dve.wait_ge(s_wt, 1)
            for n in range(3):
                last = nc.vector.tensor_copy(w_t[:, n, :], banks[n][:, 0:D])
            last.then_inc(s_wt_sb, 1)
            dve.wait_ge(s_wa, 1)
            nc.vector.tensor_copy(w_den[:, 0:D], w_in[:, 2, :])
            nc.vector.tensor_copy(w_den[:, D:DEN], banks[3][:, 0:1])
            nc.vector.tensor_copy(w_ts[:, :], banks[3][:, 0:2]).then_inc(s_wa_sb, 1)

            def half_transposed(k, n, width):
                c, half, slot = n // 2, n % 2, n % RAW
                steps = steps_of(c)
                groups = HG if half == 0 or width == IB else width // Q - HG
                off = 0 if c < NC - 1 else LOFF
                uses = k * (2 * NC // RAW) + n // RAW + 1
                dve.wait_ge(s_raw[slot], uses * (16 * A))
                if half == 0 and not (isinstance(k, int) and k * NC + c < 2):
                    dve.wait_ge(s_used, k * NC + c - 1)
                    dve.wait_ge(s_mask, k * NC + c - 1)
                g0 = half * HG
                dst = adj_t[:, c % 2, 0:steps * width].rearrange("p (s g i) -> p s g i", s=steps, i=Q)[:, :, g0:g0 + groups, :]
                src = raw[:, slot, 0:groups, off:off + steps * Q].rearrange("p g (s i) -> p s g i", i=Q)
                nc.vector.transpose(dst, src).then_inc(s_half, 1)

            def residual(k, width):
                dve.wait_ge(s_y, k + 1)
                nc.vector.tensor_tensor(yz[:, 0:width], yz[:, 0:width], x_t[:, 0:width], ALU.add).then_inc(s_z, 1)

            def centred(k, width):
                dve.wait_ge(s_mean, k + 1)
                dve.wait_ge(s_z, k + 1)
                nc.vector.tensor_tensor(zc[:, 0:width], yz[:, 0:width], ps_mean[:, 0:width], ALU.subtract).then_inc(s_zc, 1)

            def normed(k, width):
                dve.wait_ge(s_std, k + 1)
                nc.vector.reciprocal(sq[:, 0:width], sq[:, 0:width]).then_inc(s_rstd, 1)
                dve.wait_ge(s_rstd, k + 1)
                if not (isinstance(k, int) and k == 0):
                    dve.wait_ge(s_x1t, k)
                    dve.wait_ge(s_x1p, k)
                nc.vector.tensor_tensor(x1_blk[:, 0:width], zc[:, 0:width], sq[:, 0:width], ALU.mult).then_inc(s_x1, 1)

            def score_max(k, width):
                dve.wait_ge(s_tsr, k + 1)
                nc.vector.reduce_max(t_max[0:2, bass.ds(k, 1)], ts_row[0:2, 0:width], AX_X).then_inc(s_tmax, 1)
                live = width if width == IB else TAIL
                nc.vector.reduce_sum(x_sums[:, bass.ds(k, 1)], x1_blk[:, 0:live], AX_X).then_inc(s_xs, 1)

            for c in range(NC):
                n = steps_of(c)
                dve.wait_ge(s_h_ps, c + 1)
                for q in range(-(-n // 4)):
                    m = min(4, n - 4 * q)
                    last = nc.vector.tensor_tensor(h[:, c * SPC + 4 * q:c * SPC + 4 * q + m, :],
                                                   banks[6 + q][:, 0:m * D].rearrange("p (s d) -> p s d", d=D),
                                                   b_item_row[:, None, :].to_broadcast([P, m, D]), ALU.add)
                last.then_inc(s_h, 1)

            dve.wait_ge(s_pad, 2)

            def transposes(k, width, first):
                for c in range(NC):
                    half_transposed(k, 2 * c, width)
                    half_transposed(k, 2 * c + 1, width)
                    if not first:
                        if c == 1:
                            residual(k - 1, IB)
                        if c == 2:
                            centred(k - 1, IB)
                        if c == 3:
                            normed(k - 1, IB)
                        if c == NC - 1:
                            score_max(k - 1, IB)

            layer1_blocks(dve, transposes)
            residual(NB, TW)
            centred(NB, TW)
            normed(NB, TW)
            score_max(NB, TW)

            dve.wait_ge(s_tmax, NB + 1)
            nc.vector.reduce_max(t_top[:, :], t_max[0:1, :], AX_X).then_inc(s_top, 1)
            dve.wait_ge(s_topb, 1)
            nc.vector.tensor_scalar(shift[:, 1:2], ps_mean[:, 0:1], -1.0, A_SHIFT, ALU.mult, ALU.add)
            nc.vector.tensor_scalar(shift[:, 2:3], ps_mean[:, 0:1], 1.0 - SLOPE, C_SHIFT, ALU.mult, ALU.add)
            nc.vector.tensor_scalar(shift[:, 3:4], ps_mean[:, 0:1], -1.0, (F_CAP - C_SHIFT) / (1.0 - SLOPE),
                                    ALU.mult, ALU.add).then_inc(s_shift, 1)
            dve.wait_ge(s_xs, NB + 1)
            nc.vector.reduce_sum(x_sum[:, :], x_sums[:, :], AX_X).then_inc(s_xs, 1)
            def right_factor(g):
                n = min(STEPS, 3 * g + 3) - 3 * g
                dve.wait_ge(s_ac, 2 * (g + 1))
                if g == 0:
                    dve.wait_ge(s_used, NC * (NB + 1))
                ps = banks[4 + g % 4][:, 0:n * DEN].rearrange("p (s d) -> p s d", d=DEN)
                nc.vector.tensor_tensor(awh[:, 3 * g:3 * g + n, 0:D], ps[:, :, 0:D],
                                        a_col[:, 3 * g:3 * g + n, None].to_broadcast([P, n, D]), ALU.mult)
                nc.vector.tensor_copy(awh[:, 3 * g:3 * g + n, D:DEN], a_col[:, 3 * g:3 * g + n, None]).then_inc(s_awh, 1)

            def weights(k, par, width, scalar, mask, slot):
                if isinstance(k, int):
                    lhs = f_row[:, k * IB:k * IB + width]
                else:
                    lhs = f_row[:, bass.ds(k * IB, width)]
                nc.vector.scalar_tensor_tensor(out=prob[:, slot, 0:width], in0=lhs, scalar=scalar, in1=mask,
                                               op0=ALU.max, op1=ALU.mult).then_inc(s_p, 1)

            def denominators(k, width):
                nt = len(tiles_of(width))
                dve.wait_ge(s_ev, 2 * (k + 1))
                if not (isinstance(k, int) and k == 0):
                    dve.wait_ge(s_num, 3 * k)
                d_in = o_sb[:, 0:nt, D:DEN].rearrange("p t o -> p (t o)")
                nc.vector.tensor_scalar(den[:, 0, 0:nt], d_in, 0.0, None, ALU.is_equal).then_inc(s_den, 1)
                dve.wait_ge(s_den, 3 * k + 1)
                nc.vector.tensor_tensor(den[:, 1, 0:nt], den[:, 0, 0:nt], d_in, ALU.add).then_inc(s_den, 1)
                dve.wait_ge(s_den, 3 * k + 2)
                nc.vector.reciprocal(den[:, 2, 0:nt], den[:, 1, 0:nt]).then_inc(s_den, 1)

            def row_stats(k, width):
                nt = len(tiles_of(width))
                dve.wait_ge(s_zz, k + 1)
                z = el[:, 2, 0:nt * D].rearrange("p (t d) -> p t d", d=D)
                for t in range(nt):
                    last = nc.vector.bn_stats(stats[:, t, :], z[:, t, :])
                last.then_inc(s_st, 1)
                dve.wait_ge(s_st, k + 1)
                nc.vector.nop(nofuse=True)
                for t in range(nt):
                    last = nc.vector.bn_aggr(mv[:, t, :], stats[:, t, :])
                last.then_inc(s_mv, 1)

            def scaled(k, width):
                nt = len(tiles_of(width))
                z = el[:, 2, 0:nt * D].rearrange("p (t d) -> p t d", d=D)
                dve.wait_ge(s_rs, k + 1)
                nc.vector.reciprocal(rstd_o[:, 0:nt], std_o[:, 0:nt]).then_inc(s_rr, 1)
                dve.wait_ge(s_rr, k + 1)
                if not (isinstance(k, int) and k == 0):
                    dve.wait_ge(s_out, 32 * k)
                for t in range(nt):
                    last = nc.vector.tensor_scalar(o_out[:, t, :], z[:, t, :], mv[:, t, 0:1], rstd_o[:, t:t + 1],
                                                   ALU.subtract, ALU.mult)
                last.then_inc(s_fin, 1)

            def layer2(k, par, width, first):
                mask = masks[par]
                if first:
                    right_factor(0)
                    dve.wait_ge(s_f, 1)
                    dve.wait_ge(s_m0[0], 16)
                    dve.wait_ge(s_x1d, 16 * (NB + 1))
                    dve.wait_ge(s_x1t, NB + 1)
                else:
                    dve.wait_ge(s_f, 2)
                    dve.wait_ge(s_mld[par], (k + 1) * 24 if par == 1 else k * 24)
                if not (isinstance(k, int) and k == 0):
                    dve.wait_ge(s_pu, (k - 1) * STEPS + 1)
                weights(k, par, width, c_col[:, 0:1], mask[:, 0:width], UNROLL)
                if first:
                    for b in range(1, STEPS):
                        if b % 3 == 0:
                            right_factor(b // 3)
                        if b in THIRDS:
                            dve.wait_ge(s_m0[THIRDS.index(b)], 16)
                        if b > UNROLL:
                            dve.wait_ge(s_pu, b - UNROLL + 1)
                        weights(k, par, width, c_col[:, b:b + 1], mask[:, b * width:(b + 1) * width], (b - 1) % UNROLL)
                    return

                def group(g):
                    for j in range(UNROLL):
                        if isinstance(g, int) and g == 0:
                            dve.wait_ge(s_pu, k * STEPS + j + 1 - UNROLL)
                        else:
                            dve.wait_ge(s_pu, k * STEPS + g * UNROLL + j + 2 - UNROLL)
                        if isinstance(g, int):
                            b = g * UNROLL + j + 1
                            sc, mk = c_col[:, b:b + 1], mask[:, b * width:(b + 1) * width]
                        else:
                            sc = c_col[:, bass.ds(g * UNROLL + (j + 1), 1)]
                            mk = mask[:, bass.ds(g * (UNROLL * width) + (j + 1) * width, width)]
                        weights(k, par, width, sc, mk, j)

                group(0)
                denominators(k - 1, IB)
                with dve.Fori(1, GROUPS - 2) as g:
                    group(g)
                group(GROUPS - 2)
                row_stats(k - 1, IB)
                group(GROUPS - 1)
                scaled(k - 1, IB)

            layer2_blocks(dve, layer2)
            denominators(NB, TW)
            row_stats(NB, TW)
            scaled(NB, TW)

        @block.scalar
        def _(act):
            for c in range(NC):
                n = min(N, (c + 1) * JC) - c * JC
                act.wait_ge(s_item_ps, c + 1)
                if c >= 2:
                    act.wait_ge(s_h_ps, c - 1)
                for q in range(-(-n // IB)):
                    src = banks[4 + q][:, 0:min(IB, n - q * IB)]
                    if c < NC - 1:
                        to = item_t[:, c % 2, :].rearrange("p (s a j) -> p a s j", a=A, j=Q)[:, 2 * q:2 * q + 2, :, :]
                        last = nc.scalar.copy(to, src.rearrange("p (a s j) -> p a s j", a=A // 2, j=Q))
                    else:
                        if q == 0:
                            act.wait_ge(s_const, 6)
                        nc.scalar.copy(item_plain[:, q * IB:min(n, (q + 1) * IB)], src).then_inc(s_item_p, 1)
                if c == NC - 1:
                    act.wait_ge(s_item_p, 2)
                    last = in_step_order(nc.scalar.copy, item_t[:, c % 2, :], item_plain, True)[-1]
                last.then_inc(s_item_t, 1)

            def mask_chunk(k, c, width):
                act.wait_ge(s_half, k * (2 * NC) + 2 * c + 2)
                if not (isinstance(k, int) and k * NC + c < 2):
                    act.wait_ge(s_stored[c % 2], k * (8 * NC) + 16 * (c // 2))
                w = steps_of(c) * width
                nc.scalar.activation(mask_out[:, c % 2, 0:w], adj_t[:, c % 2, 0:w], ACT.Sign).then_inc(s_mask, 1)
                act.wait_ge(s_mask, k * NC + c + 1)
                act.dma_start(mask_dram[bass.ds(k, 1), :, c * SPC * width:c * SPC * width + w].rearrange("o p w -> (o p) w"),
                              mask_out[:, c % 2, 0:w]).then_inc(s_stored[c % 2], 16)

            def relu(k, width):
                act.wait_ge(s_used, NC * (k + 1))
                if not (isinstance(k, int) and k == 0):
                    act.wait_ge(s_zc, k)
                nc.scalar.activation(yz[:, 0:width], acc[:, 0:width], ACT.Relu, bias=b_user_col[:, 0:1]).then_inc(s_y, 1)

            def x_copied(k, width, live):
                act.wait_ge(s_xps, k + 1)
                if not (isinstance(k, int) and k == 0):
                    act.wait_ge(s_z, k)
                nc.scalar.copy(x_t[:, 0:live], ps_x[:, 0:live]).then_inc(s_xt, 1)

            def squares(k, width):
                act.wait_ge(s_zc, k + 1)
                if not (isinstance(k, int) and k == 0):
                    act.wait_ge(s_x1, k)
                nc.scalar.activation(sq[:, 0:width], zc[:, 0:width], ACT.Square).then_inc(s_sq, 1)

            def deviations(k, width):
                act.wait_ge(s_var, k + 1)
                nc.scalar.activation(sq[:, 0:width], ps_var[:, 0:width], ACT.Sqrt, bias=eps_col[:, 0:1]).then_inc(s_std, 1)

            def rows_out(k, width):
                act.wait_ge(s_x1p, k + 1)
                if not (isinstance(k, int) and k == 0):
                    act.wait_ge(s_x1d, 16 * k)
                    act.wait_ge(s_sd, 16 * k)
                    act.wait_ge(s_tmax, k)
                full, rest = width // P, width % P
                last = nc.scalar.copy(x1_rows[:, 0:full, :], ps_rows[:, 0:full * P].rearrange("p (t d) -> p t d", d=D))
                if rest:
                    last = nc.scalar.copy(x1_rows[0:rest, full, :], ps_rows[0:rest, full * P:full * P + D])
                last.then_inc(s_x1r, 1)
                nc.scalar.copy(ts_row[:, 0:width], ps_ts[0:2, 0:width]).then_inc(s_tsr, 1)
                act.wait_ge(s_x1r, k + 1)
                act.wait_ge(s_tsr, k + 1)
                act.dma_start(x1_dram[bass.ds(k * IB, IB), :].rearrange("(t p) d -> p t d", p=P), x1_rows[:, :, :]).then_inc(s_x1d, 16)
                act.dma_start(s_dram[:, bass.ds(k * IB, IB)], ts_row[1:2, :]).then_inc(s_sd, 16)

            def layer1(k, width, first):
                live = width if width == IB else TAIL
                if not first:
                    relu(k - 1, IB)
                else:
                    x_copied(k, width, live)
                for c in range(NC):
                    if c == 3 and not first:
                        deviations(k - 1, IB)
                    mask_chunk(k, c, width)
                    if not first:
                        if c == 0:
                            x_copied(k, width, live)
                        if c == 2:
                            squares(k - 1, IB)
                        if c == NC - 1:
                            rows_out(k - 1, IB)

            layer1_blocks(act, layer1)
            relu(NB, TW)
            squares(NB, TW)
            deviations(NB, TW)
            rows_out(NB, TW)

            act.wait_ge(s_shift, 1)

            def f_part(i, lo, hi):
                act.wait_ge(s_fcap, i + 1)
                nc.scalar.activation(f_row[:, lo:hi], f_row[:, lo:hi], ACT.Exp, bias=shift[:, 2:3], scale=1.0 - SLOPE).then_inc(s_f, 1)

            permuted = 0
            for g in range(WHG):
                n = min(STEPS, 3 * g + 3) - 3 * g
                while permuted < min(NC, (3 * (g + 3) + 2) // SPC + 1):
                    if permuted == 0:
                        act.wait_ge(s_x1t, NB + 2)
                        act.wait_ge(s_stored[0], 8 * NC * (NB + 1))
                        act.wait_ge(s_stored[1], 8 * NC * (NB + 1))
                    if permuted >= 2:
                        act.wait_ge(s_wh, (SPC * (permuted - 1) - 1) // 3 + 1)
                    done = in_step_order(nc.scalar.copy, x1_steps[:, permuted % 2, :], x1_t[:, permuted * JC:min(NP, (permuted + 1) * JC)],
                                         permuted == NC - 1)
                    done[-1].then_inc(s_perm, 1)
                    permuted += 1
                act.wait_ge(s_wh, g + 1)
                t_cols = banks[4 + g % 4][:, 0:n * DEN].rearrange("p (s d) -> p s d", d=DEN)[:, :, D:DEN]
                nc.scalar.activation(a_col[:, 3 * g:3 * g + n, None], t_cols, ACT.Exp, bias=shift[:, 1:2]).then_inc(s_ac, 1)
                nc.scalar.activation(c_col[:, 3 * g:3 * g + n, None], t_cols, ACT.Exp, bias=shift[:, 2:3],
                                     scale=-(1.0 - SLOPE)).then_inc(s_ac, 1)
                if g == 2:
                    f_part(0, 0, IB)
            f_part(1, IB, NP)
            act.wait_ge(s_whm, 1)
            nc.scalar.copy(wh_mean[:, :], banks[4][:, 0:D]).then_inc(s_wm, 1)

            def copied_out(k, par, width):
                act.wait_ge(s_pu, STEPS * (k + 1))
                if not (isinstance(k, int) and k == 0):
                    act.wait_ge(s_num, 3 * k)
                for q in range(2):
                    m = min(2, len(tiles_of(width)) - 2 * q)
                    nc.scalar.copy(o_sb[:, 2 * q:2 * q + m, :],
                                   banks[2 * par + q][:, 0:m * DEN].rearrange("p (t d) -> p t d", d=DEN)).then_inc(s_ev, 1)

            def elu_exp(k, width):
                w = len(tiles_of(width)) * D
                act.wait_ge(s_h2, 2 * k + 2)
                nc.scalar.activation(el[:, 1, 0:w], el[:, 1, 0:w], ACT.Exp).then_inc(s_exp, 1)

            def stored(k, width):
                nt = len(tiles_of(width))
                act.wait_ge(s_mv, k + 1)
                if not (isinstance(k, int) and k == 0):
                    act.wait_ge(s_fin, k)
                nc.scalar.activation(std_o[:, 0:nt], mv[:, 0:nt, 1:2].rearrange("p t o -> p (t o)"), ACT.Sqrt,
                                     bias=eps_col[:, 0:1]).then_inc(s_rs, 1)
                act.wait_ge(s_fin, k + 1)
                if width == IB:
                    rows = out[bass.ds(k * IB, IB), :].rearrange("(t p) d -> p t d", p=P)
                    for t in (0, TPB // 2):
                        act.dma_start(rows[:, t:t + TPB // 2, :], o_out[:, t:t + TPB // 2, :]).then_inc(s_out, 16)
                else:
                    full = TAIL // P
                    act.dma_start(out[NB * IB:NB * IB + full * P, :].rearrange("(t p) d -> p t d", p=P), o_out[:, 0:full, :]).then_inc(s_out, 16)
                    act.dma_start(out[NB * IB + full * P:N, :], o_out[0:TAIL - full * P, full, :]).then_inc(s_out, 16)

            def layer2(k, par, width, first):
                copied_out(k, par, width)
                elu_exp(k, width)
                stored(k, width)

            layer2_blocks(act, layer2)
            act.wait_ge(s_out, 32 * (NB + 1))


_INS = ['x', 'adj', 'L0_gnn_item_feat', 'L0_gnn_W_item', 'L0_gnn_b_item', 'L0_gnn_W_user', 'L0_gnn_b_user', 'L1_gnn_W', 'L1_gnn_a']


def kernel(**inputs):
    import numpy as _np
    import concourse.bacc as _bacc
    from concourse import mybir as _mybir
    from concourse.bass_utils import run_bass_kernel_spmd as _run

    nc = _bacc.Bacc("TRN2", target_bir_lowering=False, num_devices=1)
    arrays, args = {}, []
    for name in _INS:
        a = _np.ascontiguousarray(inputs[name])
        arrays[f"in_{name}_dram"] = a
        args.append(nc.dram_tensor(f"in_{name}_dram", a.shape, _mybir.dt.from_np(a.dtype), kind="ExternalInput").ap())
    out = nc.dram_tensor("out_0_dram", inputs['x'].shape, _mybir.dt.float32, kind="ExternalOutput").ap()
    resnorm_two_graph_layers(nc, *args, out)
    r = _run(nc, [arrays], core_ids=[0])
    return r.results[0]["out_0_dram"]
```

```python
from contextlib import ExitStack

import concourse.bass as bass
from concourse import mybir

ALU = mybir.AluOpType
ACT = mybir.ActivationFunctionType
F32 = mybir.dt.float32
U8 = mybir.dt.uint8
U32 = mybir.dt.uint32
AX_X = mybir.AxisListType.X

P = 128
D = 128
Q = 32
A = P // Q
IB = 512
TPB = IB // P
GPB = IB // Q
JC = 1024
JA = JC // A
SPC = JA // Q
HG = GPB // 2
LN_EPS = 1e-5
SLOPE = 0.2
F_CAP = 75.0
BITS = 8


def resnorm_two_graph_layers(nc, x, adj, item, w_item, b_item, w_user, b_user, w_att, a_att, out):
    N = x.shape[0]
    NB = N // IB
    TAIL = N - NB * IB
    TG = -(-TAIL // Q)
    TW = TG * Q
    NC = N // JC + 1
    LJ = (N - (NC - 1) * JC) // A
    LS = -(-LJ // Q)
    LPAD = LS * Q - LJ
    STEPS = (NC - 1) * SPC + LS
    NP = NB * IB + IB
    RAW = 5 if (2 * NC) % 5 == 0 else 4
    LOFF = JA - LJ
    RAWW = JA + LPAD
    HC = NC // 2
    DEN = D + 1
    WHG = -(-STEPS // 3)
    WHA = min(13, (NC - 1) * SPC // 3)
    assert N % A == 0 and 0 < TAIL < IB and 0 <= LPAD < Q and 0 < LJ <= JA and NC % 2 == 0 and NC >= 4
    assert (2 * NC) % RAW == 0 and NB % 2 == 1 and TG > HG
    assert SPC * D == 2 * IB and SPC == BITS and IB == 2 * JA and NB - 1 == 2 * (NC - 1)

    def steps_of(c):
        return SPC if c < NC - 1 else LS

    def cols_of(c):
        return JA if c < NC - 1 else LJ

    with ExitStack() as ctx:
        def sb(name, shape, dt=F32):
            return ctx.enter_context(nc.sbuf_tensor(name, shape, dt))

        def sem(name):
            return ctx.enter_context(nc.semaphore(name))

        mask_dram = nc.dram_tensor("mask_scratch", [NB + 1, P, NC * IB], U8, kind="Internal").ap()
        x1_dram = nc.dram_tensor("x1_scratch", [NP, D], F32, kind="Internal").ap()
        s_dram = nc.dram_tensor("s_scratch", [1, NP], F32, kind="Internal").ap()

        area_h = sb("area_h", [P, STEPS * DEN])
        h = area_h[:, 0:STEPS * D].rearrange("p (s d) -> p s d", d=D)
        awh = area_h[:, :].rearrange("p (s d) -> p s d", d=DEN)
        raw_words = RAW * HG * RAWW
        t_words = 2 * SPC * IB
        area_1 = sb("area_1", [P, max(raw_words + t_words, NP + 3 * NC * IB // 4 + 8 * IB)])
        raw = area_1[:, 0:raw_words].rearrange("p (r g w) -> p r g w", r=RAW, g=HG)
        adj_t = area_1[:, raw_words:raw_words + t_words].rearrange("p (b w) -> p b w", b=2)
        f_row = area_1[:, 0:NP]
        taken = [NP]

        def behind_f(words):
            taken[0] += words
            return area_1[:, taken[0] - words:taken[0]]

        packed_in = behind_f(2 * NC * IB // 4).rearrange("p (b w) -> p b w", b=2)
        o_sb = behind_f(TPB * DEN).rearrange("p (t d) -> p t d", d=DEN)
        el = behind_f(3 * IB).rearrange("p (b w) -> p b w", b=3)
        x1_in = behind_f(IB).rearrange("p (t d) -> p t d", d=D)
        o_out = behind_f(IB).rearrange("p (t d) -> p t d", d=D)
        area_x = sb("area_x", [P, max(NP, 7 * JC)])
        x1_t = area_x[:, 0:NP]
        item_t = area_x[:, 0:2 * JC].rearrange("p (b w) -> p b w", b=2)
        item_in = area_x[:, 2 * JC:6 * JC].rearrange("p (b t d) -> p b t d", b=4, d=D)
        item_plain = area_x[:, 6 * JC:7 * JC]

        area_m = sb("area_m", [P, 2, SPC * IB // 4])
        mask_out = area_m.bitcast(U8)
        packing = sb("packing", [P, 6 * IB // 4], U32)
        packed = sb("packed", [P, 2, HC * IB // 4], U32)
        unpacked = sb("unpacked", [P, 2, SPC, IB // 4], U32)
        x1_plain = unpacked[:, 1, :, :].rearrange("p s w -> p (s w)").bitcast(F32)
        bit_of = sb("bit_of", [P, SPC], U32)
        bit_inv = sb("bit_inv", [P, STEPS])
        table_warm = sb("table_warm", [P, 1])
        ident = sb("ident", [P, P])
        ones = sb("ones", [P, P])
        w_in = sb("w_in", [P, 3, D])
        w_t = sb("w_t", [P, 3, D])
        a_cols = sb("a_cols", [P, 2])
        w_den = sb("w_den", [P, SPC, DEN])
        w_ts = sb("w_ts", [P, 2])
        b_item_row = sb("b_item_row", [P, D])
        b_user_col = sb("b_user_col", [P, 1])
        eps_col = sb("eps_col", [P, 1])
        area_s = sb("area_s", [P, SPC, IB])
        x_in = area_s[:, 0, :].rearrange("p (t d) -> p t d", d=D)
        x_t, yz, x1_blk = (area_s[:, i, :] for i in range(1, 4))
        x1_rows = area_s[:, 4, :].rearrange("p (t d) -> p t d", d=D)
        prob = area_s
        ts_col = sb("ts_col", [P, TPB, 2])
        t_max = sb("t_max", [P, NB + 1])
        t_part = sb("t_part", [P, 1])
        t_top = sb("t_top", [1, 1])
        shift = sb("shift", [P, 4])
        a_col = sb("a_col", [P, STEPS])
        c_col = sb("c_col", [P, STEPS])
        x_sums = sb("x_sums", [P, NB + 1])
        x_sum = sb("x_sum", [P, 1])
        x_mean = sb("x_mean", [P, P])
        wh_mean = sb("wh_mean", [P, D])
        den = sb("den", [P, 3, TPB])
        stats = sb("stats", [P, TPB, 6])
        mv = sb("mv", [P, TPB, 2])
        std_o = sb("std_o", [P, TPB])
        rstd_o = sb("rstd_o", [P, TPB])

        banks = [ctx.enter_context(nc.psum_tensor(f"bank{i}", [P, IB], F32)) for i in range(8)]
        ps_x, ps_z, ps_ts, ps_back, ps_top = banks[1:6]
        acc = (banks[0], banks[6])
        item_banks = (banks[4:6], banks[2:4])
        h_banks = (banks[0:2], banks[6:8])

        s_wload = sem("s_wload")
        s_const = sem("s_const")
        s_wden = sem("s_wden")
        s_wt = sem("s_wt")
        s_wt_sb = sem("s_wt_sb")
        s_wa = sem("s_wa")
        s_wa_sb = sem("s_wa_sb")
        s_item = [sem(f"s_item{i}") for i in range(4)]
        s_item_ps = sem("s_item_ps")
        s_item_t = sem("s_item_t")
        s_h_ps = sem("s_h_ps")
        s_h = sem("s_h")
        s_pad = sem("s_pad")
        s_raw = [sem(f"s_raw{i}") for i in range(RAW)]
        s_half = sem("s_half")
        s_used = sem("s_used")
        s_mask = sem("s_mask")
        s_pk1 = sem("s_pk1")
        s_pk2 = sem("s_pk2")
        s_pk3 = sem("s_pk3")
        s_stored = [sem("s_stored0"), sem("s_stored1")]
        s_xin = sem("s_xin")
        s_xps = sem("s_xps")
        s_xt = sem("s_xt")
        s_y = sem("s_y")
        s_z = sem("s_z")
        s_zr = sem("s_zr")
        s_st1 = sem("s_st1")
        s_mv1 = sem("s_mv1")
        s_std = sem("s_std")
        s_rstd = sem("s_rstd")
        s_x1r = sem("s_x1r")
        s_x1p = sem("s_x1p")
        s_x1 = sem("s_x1")
        s_x1t = sem("s_x1t")
        s_tsp = sem("s_tsp")
        s_tsc = sem("s_tsc")
        s_tmax = sem("s_tmax")
        s_x1d = sem("s_x1d")
        s_sd = sem("s_sd")
        s_top1 = sem("s_top1")
        s_top2 = sem("s_top2")
        s_top = sem("s_top")
        s_topb = sem("s_topb")
        s_shift = sem("s_shift")
        s_plain = sem("s_plain")
        s_perm = sem("s_perm")
        s_item_p = sem("s_item_p")
        s_wh = sem("s_wh")
        s_wh_sb = sem("s_wh_sb")
        s_ac = sem("s_ac")
        s_awh = sem("s_awh")
        s_sload = [sem("s_sload0"), sem("s_sload1")]
        s_fcap = [sem("s_fcap0"), sem("s_fcap1")]
        s_f = sem("s_f")
        s_xs = sem("s_xs")
        s_xm = sem("s_xm")
        s_whm = sem("s_whm")
        s_wm = sem("s_wm")
        s_mld = [sem("s_mld0"), sem("s_mld1")]
        s_un = sem("s_un")
        s_p = sem("s_p")
        s_pu = sem("s_pu")
        s_ev = sem("s_ev")
        s_den = sem("s_den")
        s_num = sem("s_num")
        s_h2 = sem("s_h2")
        s_exp = sem("s_exp")
        s_el = sem("s_el")
        s_x1i = sem("s_x1i")
        s_zz = sem("s_zz")
        s_st = sem("s_st")
        s_mv = sem("s_mv")
        s_rs = sem("s_rs")
        s_rr = sem("s_rr")
        s_fin = sem("s_fin")
        s_out = sem("s_out")

        block = ctx.enter_context(nc.Block())

        def blocks(eng, body):
            body(0, 0, IB, True)
            body(1, 1, IB, False)
            body(2, 0, IB, False)
            with eng.Fori(3, NB - 1, 2) as k:
                body(k, 1, IB, False)
                body(k + 1, 0, IB, False)
            body(NB, 1, TW, False)

        def at(c):
            return min(c, NC - 1)

        def in_step_order(copy, dst, src, last_chunk):
            if not last_chunk:
                return [copy(dst.rearrange("p (s a j) -> p a s j", a=A, j=Q), src.rearrange("p (a s j) -> p a s j", a=A, j=Q))]
            whole = LJ // Q
            one = copy(dst[:, 0:whole * P].rearrange("p (s a j) -> p a s j", a=A, j=Q),
                       src[:, 0:A * LJ].rearrange("p (a w) -> p a w", a=A)[:, :, 0:whole * Q].rearrange("p a (s j) -> p a s j", j=Q))
            two = copy(dst[:, whole * P:(whole + 1) * P].rearrange("p (a j) -> p a j", a=A),
                       src[:, whole * Q:whole * Q + A * LJ].rearrange("p (a w) -> p a w", a=A)[:, :, 0:Q])
            return [one, two]

        def wh_bank(g):
            return (banks[7], banks[0], banks[1])[g % 3] if g < WHA else banks[4 + (g - WHA) % 4]

        def tiles_of(width):
            return [(t, min(P, width - t * P)) for t in range(-(-width // P))]

        @block.sync
        def _(sp):
            def load_item(c):
                if c >= 4:
                    sp.wait_ge(s_item_ps, c - 3)
                lo, hi = c * JC, min(N, (c + 1) * JC)
                full = (hi - lo) // P
                sp.dma_start(item_in[:, c % 4, 0:full, :], item[lo:lo + full * P, :].rearrange("(t p) d -> p t d", p=P)).then_inc(s_item[c % 4], 16)
                if hi - lo > full * P:
                    sp.dma_start(item_in[0:hi - lo - full * P, c % 4, full, :], item[lo + full * P:hi, :]).then_inc(s_item[c % 4], 16)

            load_item(0)
            for n, w in enumerate((w_item, w_user, w_att)):
                sp.dma_start(w_in[:, n, :], w).then_inc(s_wload, 16)
            sp.dma_start(a_cols[:, 0:1], a_att[0:D, :]).then_inc(s_wload, 16)
            sp.dma_start(a_cols[:, 1:2], a_att[D:2 * D, :]).then_inc(s_wload, 16)
            sp.dma_start(b_item_row[:, :], b_item.rearrange("(a d) -> a d", a=1).to_broadcast([P, D])).then_inc(s_wload, 16)
            sp.dma_start(b_user_col[:, :], b_user.rearrange("(d a) -> d a", a=1)).then_inc(s_wload, 16)
            for c in range(1, 4):
                load_item(c)

            def load_half(k, n, width):
                c, half = n // 2, n % 2
                slot = n % RAW
                groups = HG if half == 0 or width == IB else width // Q - HG
                rows = Q if half == 0 or width == IB else TAIL - HG * Q - (groups - 1) * Q
                off = 0 if c < NC - 1 else LOFF
                if not (isinstance(k, int) and k * 2 * NC + n < RAW):
                    sp.wait_ge(s_half, k * (2 * NC) + n - RAW + 1)
                for a in (0, 2, 1, 3):
                    cols = slice(c * JC + a * cols_of(c), c * JC + (a + 1) * cols_of(c))
                    if rows == Q:
                        src = adj[bass.ds(k * IB + half * HG * Q, groups * Q), cols].rearrange("(g i) w -> i g w", i=Q)
                        dst = raw[a * Q:(a + 1) * Q, slot, 0:groups, off:off + cols_of(c)]
                    else:
                        assert groups == 1
                        src = adj[N - rows:N, cols]
                        dst = raw[a * Q:a * Q + rows, slot, 0, off:off + cols_of(c)]
                    sp.dma_start(dst, src).then_inc(s_raw[slot], 16)

            def load_x(k, width):
                if not (isinstance(k, int) and k == 0):
                    sp.wait_ge(s_xps, k)
                if width == IB:
                    rows = x[bass.ds(k * IB, IB), :].rearrange("(t p) d -> p t d", p=P)
                    for t in (0, TPB // 2):
                        sp.dma_start(x_in[:, t:t + TPB // 2, :], rows[:, t:t + TPB // 2, :]).then_inc(s_xin, 16)
                else:
                    full = TAIL // P
                    sp.dma_start(x_in[:, 0:full, :], x[NB * IB:NB * IB + full * P, :].rearrange("(t p) d -> p t d", p=P)).then_inc(s_xin, 16)
                    sp.dma_start(x_in[0:TAIL - full * P, full, :], x[NB * IB + full * P:N, :]).then_inc(s_xin, 16)

            def block_loads(k, par, width, first):
                for n in range(2 * NC):
                    if first and n < RAW:
                        continue
                    if n == 0:
                        load_x(k, width)
                    load_half(k, n, width)

            load_x(0, IB)
            for c in range(4, NC):
                load_item(c)
                if c % 2 == 1:
                    load_half(0, (c - 5) // 2, IB)
            for n in range(NC // 2 - 2, RAW):
                load_half(0, n, IB)
            blocks(sp, block_loads)

            def load_mask(k, par, width):
                sp.dma_start(packed_in[:, par, 0:NC * width // 4],
                             mask_dram[bass.ds(k, 1), :, 0:NC * width].rearrange("o p w -> (o p) w").bitcast(F32)).then_inc(s_mld[par], 16)

            def load_x1(k):
                if not (isinstance(k, int) and k == 0):
                    sp.wait_ge(s_zz, k)
                sp.dma_start(x1_in[:, :, :], x1_dram[bass.ds(k * IB, IB), :].rearrange("(t p) d -> p t d", p=P)).then_inc(s_x1i, 16)

            def next_mask(k, par, width):
                sp.wait_ge(s_un, k * NC)
                load_mask(k + 1, 1 - par, width)

            sp.wait_ge(s_half, 2 * NC * (NB + 1))
            sp.wait_ge(s_used, NC * (NB + 1))
            sp.wait_ge(s_mask, NC * (NB + 1))
            sp.wait_ge(s_sd, 16 * NB)
            sp.dma_start(f_row[:, 0:IB], s_dram[:, 0:IB].to_broadcast([P, IB])).then_inc(s_sload[0], 16)
            load_mask(0, 0, IB)
            sp.wait_ge(s_sd, 16 * (NB + 1))
            sp.dma_start(f_row[:, IB:NP], s_dram[:, IB:NP].to_broadcast([P, NP - IB])).then_inc(s_sload[1], 16)
            sp.wait_ge(s_x1d, 16 * (NB + 1))
            load_x1(0)
            sp.wait_ge(s_stored[0], 16 * (NB + 1))
            sp.wait_ge(s_stored[1], 16 * (NB + 1))
            load_mask(1, 1, IB)
            next_mask(1, 1, IB)
            load_x1(1)
            next_mask(2, 0, IB)
            load_x1(2)
            with sp.Fori(3, NB - 3, 2) as k:
                next_mask(k, 1, IB)
                load_x1(k)
                next_mask(k + 1, 0, IB)
                load_x1(k + 1)
            next_mask(NB - 2, 1, IB)
            load_x1(NB - 2)
            next_mask(NB - 1, 0, TW)
            load_x1(NB - 1)
            load_x1(NB)

        @block.gpsimd
        def _(pool):
            nc.gpsimd.memset(ones[:, :], 1.0).then_inc(s_const, 1)
            nc.gpsimd.memset(ident[:, :], 0.0).then_inc(s_const, 1)
            pool.wait_ge(s_const, 2)
            nc.gpsimd.affine_select(out=ident[:, :], in_=ident[:, :], compare_op=ALU.not_equal, fill=1.0, base=0,
                                    pattern=[[-1, P]], channel_multiplier=1).then_inc(s_const, 1)
            for n in range(SPC):
                bit = 1 << (SPC - 1 - n)
                nc.gpsimd.memset(bit_of.bitcast(U8)[:, 4 * n:4 * n + 4], bit)
                last = nc.gpsimd.memset(bit_inv[:, n:STEPS:SPC], 1.0 / bit)
            last.then_inc(s_const, 1)
            nc.gpsimd.memset(item_plain[:, :], 0.0).then_inc(s_const, 1)
            nc.gpsimd.memset(eps_col[:, :], LN_EPS).then_inc(s_const, 1)
            for n in (2 * NC - 2, 2 * NC - 1):
                nc.gpsimd.memset(raw[:, n % RAW, :, JA:RAWW], 0.0).then_inc(s_pad, 1)

            last_chunk = x1_t[:, (NC - 1) * JC:NC * JC]

            def keep_x1(k, par, width, first):
                if width == IB:
                    chunk = x1_t[:, bass.ds((k - par) * IB, JC)].rearrange("p (s a j) -> p a s j", a=A, j=Q)
                    pool.wait_ge(s_x1, k + 1)
                    nc.gpsimd.tensor_copy(chunk[:, 2 * par:2 * par + 2, :, :],
                                          x1_blk.rearrange("p (a s j) -> p a s j", a=2, j=Q)).then_inc(s_x1t, 1)
                else:
                    pool.wait_ge(s_x1t, NB)
                    nc.gpsimd.tensor_copy(x1_plain[:, 0:IB].rearrange("p (a s j) -> p a s j", a=2, j=Q),
                                          last_chunk.rearrange("p (s a j) -> p a s j", a=A, j=Q)[:, 0:2, :, :]).then_inc(s_plain, 1)
                    nc.gpsimd.memset(x1_plain[:, IB + TW:IB + TW + Q], 0.0).then_inc(s_plain, 1)
                    pool.wait_ge(s_x1, k + 1)
                    nc.gpsimd.tensor_copy(x1_plain[:, IB:IB + width], x1_blk[:, 0:width]).then_inc(s_x1t, 1)

            blocks(pool, keep_x1)
            pool.wait_ge(s_plain, 2)
            pool.wait_ge(s_x1t, NB + 1)
            in_step_order(nc.gpsimd.tensor_copy, last_chunk[:, 0:LS * P], x1_plain, True)[-1].then_inc(s_perm, 1)

            pool.wait_ge(s_shift, 1)
            pool.wait_ge(s_sload[1], 16)
            nc.gpsimd.tensor_scalar(f_row[:, IB:NP], f_row[:, IB:NP], shift[:, 2:3], None, ALU.min).then_inc(s_fcap[1], 1)
            pool.wait_ge(s_xs, NB + 2)
            nc.gpsimd.tensor_scalar(x_mean[:, :], ones[:, :], x_sum[:, 0:1], 1.0 / N, ALU.mult, ALU.mult).then_inc(s_xm, 1)

            def epilogue(k, par, width, first):
                nt = len(tiles_of(width))
                w = nt * D
                num = o_sb[:, 0:nt, 0:D]
                e0, e1, e2 = (el[:, i, 0:w].rearrange("p (t d) -> p t d", d=D) for i in range(3))
                if first:
                    pool.wait_ge(s_wm, 1)
                pool.wait_ge(s_den, 3 * (k + 1))
                nc.gpsimd.tensor_tensor(e0, wh_mean[:, None, :].to_broadcast([P, nt, D]),
                                        den[:, 0, 0:nt, None].to_broadcast([P, nt, D]), ALU.mult).then_inc(s_num, 1)
                pool.wait_ge(s_num, 3 * k + 1)
                nc.gpsimd.tensor_tensor(e1, e0, num, ALU.add).then_inc(s_num, 1)
                pool.wait_ge(s_num, 3 * k + 2)
                nc.gpsimd.tensor_tensor(e0, e1, den[:, 2, 0:nt, None].to_broadcast([P, nt, D]), ALU.mult).then_inc(s_num, 1)
                pool.wait_ge(s_num, 3 * k + 3)
                nc.gpsimd.nop(nofuse=True)
                nc.gpsimd.tensor_scalar(el[:, 1, 0:w], el[:, 0, 0:w], 0.0, None, ALU.min).then_inc(s_h2, 1)
                if not (isinstance(k, int) and k == 0):
                    pool.wait_ge(s_fin, k)
                    nc.gpsimd.nop(nofuse=True)
                nc.gpsimd.tensor_scalar(el[:, 2, 0:w], el[:, 0, 0:w], 0.0, -1.0, ALU.max, ALU.add).then_inc(s_h2, 1)
                pool.wait_ge(s_exp, k + 1)
                pool.wait_ge(s_h2, 2 * k + 2)
                nc.gpsimd.tensor_tensor(el[:, 0, 0:w], el[:, 1, 0:w], el[:, 2, 0:w], ALU.add).then_inc(s_el, 1)
                pool.wait_ge(s_el, k + 1)
                pool.wait_ge(s_x1i, 16 * (k + 1))
                nc.gpsimd.tensor_tensor(e2, e0, x1_in[:, 0:nt, :], ALU.add).then_inc(s_zz, 1)

            def layer2(k, par, width, first):
                epilogue(k, par, width, first)

            blocks(pool, layer2)

        @block.tensor
        def _(pe):
            def item_transposes(c):
                n = min(N, (c + 1) * JC) - c * JC
                pe.wait_ge(s_item[c % 4], 16 * (c // 4 + 1) if c < NC - 1 else 16 * (c // 4 + 2))
                if c == 1:
                    pe.wait_ge(s_wa_sb, 1)
                if c >= 2:
                    pe.wait_ge(s_item_t, c - 1)
                for t in range(-(-n // P)):
                    m = min(P, n - t * P)
                    mm = nc.tensor.transpose(item_banks[c % 2][t // 4][:, (t % 4) * P:(t % 4) * P + m],
                                             item_in[0:m, c % 4, t, :], ident[0:m, 0:m])
                mm.then_inc(s_item_ps, 1)

            def h_products(c):
                pe.wait_ge(s_item_t, c + 1)
                if c >= 2:
                    pe.wait_ge(s_h, c - 1)
                for s in range(steps_of(c)):
                    mm = nc.tensor.matmul(h_banks[c % 2][s // 4][:, (s % 4) * D:(s % 4 + 1) * D],
                                          item_t[:, c % 2, s * P:(s + 1) * P], w_t[:, 0, :], start=True, stop=True)
                mm.then_inc(s_h_ps, 1)

            pe.wait_ge(s_const, 3)
            item_transposes(0)
            pe.wait_ge(s_wload, 16 * 7)
            for n in range(3):
                mm = nc.tensor.transpose(banks[n][:, 0:D], w_in[:, n, :], ident[:, :])
            mm.then_inc(s_wt, 1)
            pe.wait_ge(s_wt_sb, 1)
            nc.tensor.matmul(banks[3][:, 0:1], w_t[:, 2, :], a_cols[:, 1:2], start=True, stop=True)
            nc.tensor.matmul(banks[3][:, 1:2], w_t[:, 2, :], a_cols[:, 0:1], start=True, stop=True).then_inc(s_wa, 1)
            for c in range(NC):
                if c + 1 < NC:
                    item_transposes(c + 1)
                h_products(c)

            def z_rows(k, width):
                pe.wait_ge(s_z, k + 1)
                if not (isinstance(k, int) and k == 0):
                    pe.wait_ge(s_x1r, k)
                for t, m in tiles_of(width):
                    mm = nc.tensor.transpose(ps_z[0:m, t * P:t * P + D], yz[:, t * P:t * P + m], ident[:, :])
                mm.then_inc(s_zr, 1)

            def x1_back(k, width):
                pe.wait_ge(s_x1r, k + 1)
                if not (isinstance(k, int) and k == 0):
                    pe.wait_ge(s_x1, k)
                for t, m in tiles_of(width):
                    mm = nc.tensor.transpose(ps_back[:, t * P:t * P + m], x1_rows[0:m, t, :], ident[0:m, 0:m])
                mm.then_inc(s_x1p, 1)

            def score_parts(k, width):
                pe.wait_ge(s_x1, k + 1)
                if not (isinstance(k, int) and k == 0):
                    pe.wait_ge(s_tsc, k)
                for t, m in tiles_of(width):
                    mm = nc.tensor.matmul(ps_ts[0:m, 2 * t:2 * t + 2], x1_blk[:, t * P:t * P + m], w_ts[:, :], start=True, stop=True)
                mm.then_inc(s_tsp, 1)

            def contract(k, par, width, first):
                pe.wait_ge(s_xin, 32 * (k + 1))
                if not first:
                    pe.wait_ge(s_xt, k)
                live = tiles_of(width) if width == IB else tiles_of(TAIL)
                for t, m in live:
                    mm = nc.tensor.transpose(ps_x[:, t * P:t * P + m], x_in[0:m, t, :], ident[0:m, 0:m])
                mm.then_inc(s_xps, 1)
                for c in range(NC):
                    if first and c == 1:
                        pe.wait_ge(s_h, NC)
                    pe.wait_ge(s_half, k * (2 * NC) + 2 * c + 2)
                    if c == 0 and not (isinstance(k, int) and k < 2):
                        pe.wait_ge(s_y, k - 1)
                    if c == at(4):
                        pe.wait_ge(s_xt, k + 1)
                        nc.tensor.matmul(acc[par][:, 0:width], w_t[:, 1, :], x_t[:, 0:width], start=False, stop=False)
                    for s in range(steps_of(c)):
                        mm = nc.tensor.matmul(acc[par][:, 0:width], h[:, c * SPC + s, :],
                                              adj_t[:, c % 2, s * width:(s + 1) * width],
                                              start=(c == 0 and s == 0), stop=(c == NC - 1 and s == LS - 1))
                    mm.then_inc(s_used, 1)
                    if not first:
                        if c == 1:
                            z_rows(k - 1, IB)
                        if c == at(4):
                            x1_back(k - 1, IB)
                        if c == at(5):
                            score_parts(k - 1, IB)

            pe.wait_ge(s_h, NC - 1)
            blocks(pe, contract)

            def wh_products(g):
                before = [f for f in range(g) if wh_bank(f) is wh_bank(g)]
                if before:
                    pe.wait_ge(s_wh_sb, before[-1] + 1)
                for b in range(3 * g, min(STEPS, 3 * g + 3)):
                    if b == (NC - 1) * SPC:
                        pe.wait_ge(s_perm, 1)
                    mm = nc.tensor.matmul(wh_bank(g)[:, (b - 3 * g) * DEN:(b - 3 * g + 1) * DEN],
                                          x1_t[:, b * P:(b + 1) * P], w_den[:, b % SPC, :], start=True, stop=True)
                mm.then_inc(s_wh, 1)

            def some_wh(lo, hi):
                for g in range(lo, min(hi, WHA)):
                    wh_products(g)

            pe.wait_ge(s_x1t, NB - 1)
            pe.wait_ge(s_y, NB)
            pe.wait_ge(s_wden, 1)
            some_wh(0, 2)
            z_rows(NB, TW)
            some_wh(2, 5)
            x1_back(NB, TW)
            some_wh(5, 7)
            score_parts(NB, TW)
            some_wh(7, 10)
            pe.wait_ge(s_top1, 1)
            nc.tensor.transpose(ps_top[0:1, 0:P], t_part[:, :], ident[:, :]).then_inc(s_top2, 1)
            some_wh(10, 11)
            pe.wait_ge(s_top, 1)
            nc.tensor.matmul(ps_top[:, P:P + 1], ones[0:1, :], t_top[0:1, 0:1], start=True, stop=True).then_inc(s_topb, 1)
            some_wh(11, WHA)
            pe.wait_ge(s_x1, NB + 1)
            pe.wait_ge(s_shift, 1)
            pe.wait_ge(s_wh_sb, WHA)

            def weighted(par, width, right, slot, start, stop):
                for t, m in tiles_of(width):
                    bank = banks[2 * par + t // 2]
                    mm = nc.tensor.matmul(bank[0:m, (t % 2) * DEN:(t % 2 + 1) * DEN], prob[:, slot, t * P:t * P + m],
                                          right, start=start and t % 2 == 0, stop=stop, skip_group_check=True)
                mm.then_inc(s_pu, 1)

            def layer2(k, par, width, first):
                if not (isinstance(k, int) and k < 2):
                    pe.wait_ge(s_ev, 2 * (k - 1))
                def chunk(c, first_block=False):
                    for n in range(steps_of(c) if isinstance(c, int) else SPC):
                        b = c * SPC + n
                        if first_block and b % 3 == 0 and WHA <= b // 3 + 3 < WHG:
                            wh_products(b // 3 + 3)
                        if first_block:
                            pe.wait_ge(s_awh, b // 3 + 1)
                        pe.wait_ge(s_p, k * STEPS + b + 1)
                        if isinstance(c, int):
                            right = awh[:, b, :]
                        else:
                            right = area_h[:, bass.ds(c * (SPC * DEN) + n * DEN, DEN)]
                        weighted(par, width, right, n, isinstance(b, int) and b == 0, isinstance(b, int) and b == STEPS - 1)

                if first:
                    for c in range(NC):
                        chunk(c, True)
                    pe.wait_ge(s_xm, 1)
                    nc.tensor.matmul(banks[4][:, 0:D], x_mean[:, :], w_in[:, 2, :], start=True, stop=True).then_inc(s_whm, 1)
                    return
                chunk(0)
                with pe.Fori(1, NC - 1) as c:
                    chunk(c)
                chunk(NC - 1)

            blocks(pe, layer2)

        @block.vector
        def _(dve):
            dve.wait_ge(s_wt, 1)
            for n in range(3):
                last = nc.vector.tensor_copy(w_t[:, n, :], banks[n][:, 0:D])
            last.then_inc(s_wt_sb, 1)
            dve.wait_ge(s_wa, 1)
            nc.vector.tensor_copy(w_ts[:, :], banks[3][:, 0:2]).then_inc(s_wa_sb, 1)

            def half_transposed(k, n, width):
                c, half, slot = n // 2, n % 2, n % RAW
                steps = steps_of(c)
                groups = HG if half == 0 or width == IB else width // Q - HG
                off = 0 if c < NC - 1 else LOFF
                uses = k * (2 * NC // RAW) + n // RAW + 1
                dve.wait_ge(s_raw[slot], uses * (16 * A))
                if half == 0 and not (isinstance(k, int) and k * NC + c < 2):
                    dve.wait_ge(s_used, k * NC + c - 1)
                    dve.wait_ge(s_mask, k * NC + c - 1)
                g0 = half * HG
                dst = adj_t[:, c % 2, 0:steps * width].rearrange("p (s g i) -> p s g i", s=steps, i=Q)[:, :, g0:g0 + groups, :]
                src = raw[:, slot, 0:groups, off:off + steps * Q].rearrange("p g (s i) -> p s g i", i=Q)
                nc.vector.transpose(dst, src).then_inc(s_half, 1)

            def residual(k, width):
                dve.wait_ge(s_y, k + 1)
                nc.vector.tensor_tensor(yz[:, 0:width], yz[:, 0:width], x_t[:, 0:width], ALU.add).then_inc(s_z, 1)

            def row_stats1(k, width):
                dve.wait_ge(s_zr, k + 1)
                tiles = tiles_of(width)
                for t, m in tiles:
                    last = nc.vector.bn_stats(stats[0:m, t, :], ps_z[0:m, t * P:t * P + D])
                last.then_inc(s_st1, 1)
                dve.wait_ge(s_st1, k + 1)
                nc.vector.nop(nofuse=True)
                for t, m in tiles:
                    last = nc.vector.bn_aggr(mv[0:m, t, :], stats[0:m, t, :])
                last.then_inc(s_mv1, 1)

            def normed(k, width):
                dve.wait_ge(s_std, k + 1)
                tiles = tiles_of(width)
                nc.vector.reciprocal(rstd_o[:, 0:len(tiles)], std_o[:, 0:len(tiles)]).then_inc(s_rstd, 1)
                dve.wait_ge(s_rstd, k + 1)
                if not (isinstance(k, int) and k == 0):
                    dve.wait_ge(s_x1p, k)
                    dve.wait_ge(s_x1d, 16 * k)
                for t, m in tiles:
                    last = nc.vector.tensor_scalar(x1_rows[0:m, t, :], ps_z[0:m, t * P:t * P + D], mv[0:m, t, 0:1],
                                                   rstd_o[0:m, t:t + 1], ALU.subtract, ALU.mult)
                last.then_inc(s_x1r, 1)

            def block_sums(k, width):
                dve.wait_ge(s_tsc, k + 1)
                nc.vector.reduce_max(t_max[:, bass.ds(k, 1)], ts_col[:, 0:len(tiles_of(width)), 0], AX_X).then_inc(s_tmax, 1)
                live = width if width == IB else TAIL
                nc.vector.reduce_sum(x_sums[:, bass.ds(k, 1)], x1_blk[:, 0:live], AX_X).then_inc(s_xs, 1)

            packs = packing[:, :].rearrange("p (s w) -> p s w", w=IB // 4)

            def pack1(k, c, width):
                dve.wait_ge(s_mask, k * NC + c + 1)
                w = width // 4
                m = mask_out[:, c % 2, 0:SPC * width].bitcast(U32).rearrange("p (s w) -> p s w", s=SPC)
                nc.vector.scalar_tensor_tensor(out=packs[:, 0:4, 0:w], in0=m[:, 0:4, :], scalar=4, in1=m[:, 4:8, :],
                                               op0=ALU.logical_shift_left, op1=ALU.bitwise_or).then_inc(s_pk1, 1)

            def pack2(k, c, width):
                dve.wait_ge(s_pk1, k * NC + c + 1)
                w = width // 4
                nc.vector.scalar_tensor_tensor(out=packs[:, 4:6, 0:w], in0=packs[:, 0:2, 0:w], scalar=2, in1=packs[:, 2:4, 0:w],
                                               op0=ALU.logical_shift_left, op1=ALU.bitwise_or).then_inc(s_pk2, 1)

            def pack3(k, c, width):
                dve.wait_ge(s_pk2, k * NC + c + 1)
                if c % HC == 0 and not (isinstance(k, int) and k == 0):
                    dve.wait_ge(s_stored[c // HC], 16 * k)
                w = width // 4
                nc.vector.scalar_tensor_tensor(out=packed[:, c // HC, (c % HC) * w:(c % HC + 1) * w], in0=packs[:, 4, 0:w], scalar=1,
                                               in1=packs[:, 5, 0:w], op0=ALU.logical_shift_left, op1=ALU.bitwise_or).then_inc(s_pk3, 1)

            EARLY = (NC - 3, NC - 1)
            for c in range(NC):
                if c == 1:
                    dve.wait_ge(s_const, 4)
                    dve.wait_ge(s_wa_sb, 1)
                    for n in range(SPC):
                        nc.vector.tensor_scalar(w_den[:, n, 0:D], w_in[:, 2, :], bit_inv[:, n:n + 1], None, ALU.mult)
                        last = nc.vector.tensor_copy(w_den[:, n, D:DEN], w_ts[:, 0:1])
                    last.then_inc(s_wden, 1)
                if c in EARLY:
                    half_transposed(0, EARLY.index(c), IB)
                n = steps_of(c)
                dve.wait_ge(s_h_ps, c + 1)
                for q in range(-(-n // 4)):
                    m = min(4, n - 4 * q)
                    last = nc.vector.tensor_tensor(h[:, c * SPC + 4 * q:c * SPC + 4 * q + m, :],
                                                   h_banks[c % 2][q][:, 0:m * D].rearrange("p (s d) -> p s d", d=D),
                                                   b_item_row[:, None, :].to_broadcast([P, m, D]), ALU.add)
                last.then_inc(s_h, 1)

            dve.wait_ge(s_pad, 2)

            def transposes(k, par, width, first):
                for c in range(NC):
                    one = (k, c - 1, width) if c >= 1 else (k - 1, NC - 1, IB)
                    two = (k, c - 2, width) if c >= 2 else (k - 1, NC + c - 2, IB)
                    if not first or 2 * c >= len(EARLY):
                        half_transposed(k, 2 * c, width)
                    if not first or c >= 2:
                        pack2(*two)
                    if not first or 2 * c + 1 >= len(EARLY):
                        half_transposed(k, 2 * c + 1, width)
                    if not first or c >= 2:
                        pack3(*two)
                    if not first or c >= 1:
                        pack1(*one)
                    if not first:
                        if c == 2:
                            residual(k - 1, IB)
                        if c == at(3):
                            row_stats1(k - 1, IB)
                        if c == at(4):
                            normed(k - 1, IB)
                        if c == NC - 1:
                            block_sums(k - 1, IB)

            blocks(dve, transposes)
            residual(NB, TW)
            row_stats1(NB, TW)
            normed(NB, TW)
            block_sums(NB, TW)

            dve.wait_ge(s_tmax, NB + 1)
            nc.vector.reduce_max(t_part[:, :], t_max[:, :], AX_X).then_inc(s_top1, 1)
            pack2(NB, NC - 2, TW)
            pack3(NB, NC - 2, TW)
            pack1(NB, NC - 1, TW)
            dve.wait_ge(s_top2, 1)
            nc.vector.reduce_max(t_top[:, :], ps_top[0:1, 0:P], AX_X).then_inc(s_top, 1)
            pack2(NB, NC - 1, TW)
            pack3(NB, NC - 1, TW)
            dve.wait_ge(s_topb, 1)
            top = ps_top[:, P:P + 1]
            nc.vector.tensor_scalar(shift[:, 0:1], top, -1.0, None, ALU.mult)
            nc.vector.tensor_scalar(shift[:, 1:2], top, 1.0 - SLOPE, None, ALU.mult)
            nc.vector.tensor_scalar(shift[:, 2:3], top, -1.0, F_CAP / (1.0 - SLOPE), ALU.mult, ALU.add).then_inc(s_shift, 1)
            dve.wait_ge(s_sload[0], 16)
            dve.wait_ge(s_shift, 1)
            nc.vector.tensor_scalar(f_row[:, 0:IB], f_row[:, 0:IB], shift[:, 2:3], None, ALU.min).then_inc(s_fcap[0], 1)
            dve.wait_ge(s_xs, NB + 1)
            nc.vector.reduce_sum(x_sum[:, :], x_sums[:, :], AX_X).then_inc(s_xs, 1)

            def right_factor(g):
                n = min(STEPS, 3 * g + 3) - 3 * g
                dve.wait_ge(s_ac, 2 * (max(0, g - WHA + 1) + 1))
                mine = awh[:, 3 * g:3 * g + n, 0:D]
                a = a_col[:, 3 * g:3 * g + n, None]
                nc.vector.tensor_tensor(mine, mine, a.to_broadcast([P, n, D]), ALU.mult)
                nc.vector.tensor_tensor(awh[:, 3 * g:3 * g + n, D:DEN], a, bit_inv[:, 3 * g:3 * g + n, None], ALU.mult).then_inc(s_awh, 1)

            def weights(k, par, width, scalar, mask, slot):
                if isinstance(k, int):
                    lhs = f_row[:, k * IB:k * IB + width]
                else:
                    lhs = f_row[:, bass.ds(k * IB, width)]
                nc.vector.scalar_tensor_tensor(out=prob[:, slot, 0:width], in0=lhs, scalar=scalar, in1=mask,
                                               op0=ALU.max, op1=ALU.mult).then_inc(s_p, 1)

            def denominators(k, width):
                nt = len(tiles_of(width))
                dve.wait_ge(s_ev, 2 * (k + 1))
                if not (isinstance(k, int) and k == 0):
                    dve.wait_ge(s_num, 3 * k)
                d_in = o_sb[:, 0:nt, D:DEN].rearrange("p t o -> p (t o)")
                nc.vector.tensor_scalar(den[:, 0, 0:nt], d_in, 0.0, None, ALU.is_equal).then_inc(s_den, 1)
                dve.wait_ge(s_den, 3 * k + 1)
                nc.vector.tensor_tensor(den[:, 1, 0:nt], den[:, 0, 0:nt], d_in, ALU.add).then_inc(s_den, 1)
                dve.wait_ge(s_den, 3 * k + 2)
                nc.vector.reciprocal(den[:, 2, 0:nt], den[:, 1, 0:nt]).then_inc(s_den, 1)

            def row_stats(k, width):
                nt = len(tiles_of(width))
                dve.wait_ge(s_zz, k + 1)
                z = el[:, 2, 0:nt * D].rearrange("p (t d) -> p t d", d=D)
                for t in range(nt):
                    last = nc.vector.bn_stats(stats[:, t, :], z[:, t, :])
                last.then_inc(s_st, 1)
                dve.wait_ge(s_st, k + 1)
                nc.vector.nop(nofuse=True)
                for t in range(nt):
                    last = nc.vector.bn_aggr(mv[:, t, :], stats[:, t, :])
                last.then_inc(s_mv, 1)

            def scaled(k, width):
                nt = len(tiles_of(width))
                z = el[:, 2, 0:nt * D].rearrange("p (t d) -> p t d", d=D)
                dve.wait_ge(s_rs, k + 1)
                nc.vector.reciprocal(rstd_o[:, 0:nt], std_o[:, 0:nt]).then_inc(s_rr, 1)
                dve.wait_ge(s_rr, k + 1)
                if not (isinstance(k, int) and k == 0):
                    dve.wait_ge(s_out, 32 * k)
                for t in range(nt):
                    last = nc.vector.tensor_scalar(o_out[:, t, :], z[:, t, :], mv[:, t, 0:1], rstd_o[:, t:t + 1],
                                                   ALU.subtract, ALU.mult)
                last.then_inc(s_fin, 1)

            def unpack(k, par, width, c, slot):
                w = width // 4
                if isinstance(c, int):
                    if c == 0:
                        dve.wait_ge(s_mld[par], (k + 1) * 8 if par == 1 else (k + 2) * 8)
                    if not (isinstance(k, int) and k == 0 and c < 2):
                        dve.wait_ge(s_p, k * STEPS + ((c - 1) * SPC if c > 0 else -LS))
                    if isinstance(k, int) and k == 0 and c == 1:
                        dve.wait_ge(s_perm, 1)
                    src = packed_in[:, par, c * w:(c + 1) * w]
                    n = steps_of(c)
                else:
                    dve.wait_ge(s_p, k * STEPS + (c - 1) * SPC)
                    src = packed_in[:, par, bass.ds(c * w, w)]
                    n = SPC
                nc.vector.tensor_tensor(unpacked[:, slot, 0:n, 0:w], src.bitcast(U32)[:, None, :].to_broadcast([P, n, w]),
                                        bit_of[:, 0:n, None].to_broadcast([P, n, w]), ALU.bitwise_and).then_inc(s_un, 1)

            def layer2(k, par, width, first):
                if first:
                    unpack(0, 0, IB, 0, 0)
                    right_factor(0)
                    dve.wait_ge(s_f, 1)
                    dve.wait_ge(s_x1d, 16 * (NB + 1))
                    dve.wait_ge(s_x1t, NB + 1)
                    dve.wait_ge(s_tsp, NB + 1)
                else:
                    dve.wait_ge(s_f, 2)

                def chunk(c, slot):
                    dve.wait_ge(s_un, k * NC + c + 1)
                    for n in range(steps_of(c) if isinstance(c, int) else SPC):
                        b = c * SPC + n
                        if first and b % 3 == 0 and b > 0:
                            right_factor(b // 3)
                        if not isinstance(c, int) or c > 0:
                            dve.wait_ge(s_pu, k * STEPS + b - SPC + 1)
                        elif not first:
                            dve.wait_ge(s_pu, k * STEPS + (n - LS + 1 if n < LS else n - LS - SPC + 1))
                        if isinstance(c, int):
                            scalar = c_col[:, b:b + 1]
                        else:
                            scalar = c_col[:, bass.ds(c * SPC + n, 1)]
                        weights(k, par, width, scalar, unpacked[:, slot, n, 0:width // 4].bitcast(U8), n)
                        if n == 2:
                            if not isinstance(c, int) or c < NC - 1:
                                unpack(k, par, width, c + 1, 1 - slot)
                            elif not (isinstance(k, int) and k == NB):
                                unpack(k + 1, 1 - par, IB, 0, 0)

                if first:
                    for c in range(NC):
                        chunk(c, c % 2)
                    return
                chunk(0, 0)
                denominators(k - 1, IB)
                with dve.Fori(1, NC - 2, 2) as c:
                    chunk(c, 1)
                    chunk(c + 1, 0)
                row_stats(k - 1, IB)
                chunk(NC - 1, 1)
                scaled(k - 1, IB)

            blocks(dve, layer2)
            denominators(NB, TW)
            row_stats(NB, TW)
            scaled(NB, TW)

        @block.scalar
        def _(act):
            for c in range(NC):
                n = min(N, (c + 1) * JC) - c * JC
                act.wait_ge(s_item_ps, c + 1)
                if c >= 2:
                    act.wait_ge(s_h_ps, c - 1)
                for q in range(-(-n // IB)):
                    src = item_banks[c % 2][q][:, 0:min(IB, n - q * IB)]
                    if c < NC - 1:
                        to = item_t[:, c % 2, :].rearrange("p (s a j) -> p a s j", a=A, j=Q)[:, 2 * q:2 * q + 2, :, :]
                        last = nc.scalar.copy(to, src.rearrange("p (a s j) -> p a s j", a=A // 2, j=Q))
                    else:
                        if q == 0:
                            act.wait_ge(s_const, 6)
                        nc.scalar.copy(item_plain[:, q * IB:min(n, (q + 1) * IB)], src).then_inc(s_item_p, 1)
                if c == NC - 1:
                    act.wait_ge(s_item_p, 2)
                    last = in_step_order(nc.scalar.copy, item_t[:, c % 2, :], item_plain, True)[-1]
                last.then_inc(s_item_t, 1)

            def mask_chunk(k, c, width):
                act.wait_ge(s_half, k * (2 * NC) + 2 * c + 2)
                if not (isinstance(k, int) and k * NC + c < 2):
                    act.wait_ge(s_pk1, k * NC + c - 1)
                w = steps_of(c) * width
                nc.scalar.activation(mask_out[:, c % 2, 0:w], adj_t[:, c % 2, 0:w], ACT.Sign).then_inc(s_mask, 1)

            def store_masks(k, half, width):
                act.wait_ge(s_pk3, k * NC + (half + 1) * HC)
                lo, hi = half * HC * width, (half + 1) * HC * width
                act.dma_start(mask_dram[bass.ds(k, 1), :, lo:hi].rearrange("o p w -> (o p) w").bitcast(U32),
                              packed[:, half, 0:HC * width // 4]).then_inc(s_stored[half], 16)

            def relu(k, par, width):
                act.wait_ge(s_used, NC * (k + 1))
                if not (isinstance(k, int) and k == 0):
                    act.wait_ge(s_zr, k)
                nc.scalar.activation(yz[:, 0:width], acc[par][:, 0:width], ACT.Relu, bias=b_user_col[:, 0:1]).then_inc(s_y, 1)

            def x_copied(k, width, live):
                act.wait_ge(s_xps, k + 1)
                if not (isinstance(k, int) and k == 0):
                    act.wait_ge(s_z, k)
                nc.scalar.copy(x_t[:, 0:live], ps_x[:, 0:live]).then_inc(s_xt, 1)

            def deviations(k, width):
                nt = len(tiles_of(width))
                act.wait_ge(s_mv1, k + 1)
                if not (isinstance(k, int) and k == 0):
                    act.wait_ge(s_rstd, k)
                nc.scalar.activation(std_o[:, 0:nt], mv[:, 0:nt, 1:2].rearrange("p t o -> p (t o)"), ACT.Sqrt,
                                     bias=eps_col[:, 0:1]).then_inc(s_std, 1)

            def x1_stored(k):
                act.wait_ge(s_x1r, k + 1)
                act.dma_start(x1_dram[bass.ds(k * IB, IB), :].rearrange("(t p) d -> p t d", p=P), x1_rows[:, :, :]).then_inc(s_x1d, 16)

            def x1_copied(k, width):
                act.wait_ge(s_x1p, k + 1)
                if not (isinstance(k, int) and k == 0):
                    act.wait_ge(s_x1t, k)
                    act.wait_ge(s_tsp, k)
                    act.wait_ge(s_xs, k)
                nc.scalar.copy(x1_blk[:, 0:width], ps_back[:, 0:width]).then_inc(s_x1, 1)

            def scores_out(k, width):
                act.wait_ge(s_tsp, k + 1)
                if not (isinstance(k, int) and k == 0):
                    act.wait_ge(s_sd, 16 * k)
                    act.wait_ge(s_tmax, k)
                for t, m in tiles_of(width):
                    if t == 0 or m < P:
                        n = width // P if t == 0 else 1
                        last = nc.scalar.copy(ts_col[0:m, t:t + n, :], ps_ts[0:m, 2 * t:2 * t + 2 * n].rearrange("p (t o) -> p t o", o=2))
                last.then_inc(s_tsc, 1)
                act.wait_ge(s_tsc, k + 1)
                with nc.allow_non_contiguous_dma(reason="one word for each row of the block"):
                    act.dma_start(s_dram[:, bass.ds(k * IB, IB)].rearrange("o (t p w) -> p (o t) w", p=P, w=1), ts_col[:, :, 1:2]).then_inc(s_sd, 16)

            def layer1(k, par, width, first):
                live = width if width == IB else TAIL
                if first:
                    x_copied(k, width, live)
                for c in range(NC):
                    mask_chunk(k, c, width)
                    if not first:
                        if c == 0:
                            relu(k - 1, 1 - par, IB)
                        if c == 1:
                            store_masks(k - 1, 1, IB)
                        if c == at(3):
                            x_copied(k, width, live)
                            deviations(k - 1, IB)
                        if c == at(4):
                            x1_stored(k - 1)
                        if c == at(5):
                            x1_copied(k - 1, IB)
                        if c == at(7):
                            scores_out(k - 1, IB)
                    if c == HC + 1:
                        store_masks(k, 0, width)

            blocks(act, layer1)

            def wh_copied(lo, hi):
                for g in range(lo, min(hi, WHG)):
                    n = min(STEPS, 3 * g + 3) - 3 * g
                    act.wait_ge(s_wh, g + 1)
                    nc.scalar.copy(area_h[:, 3 * g * DEN:(3 * g + n) * DEN], wh_bank(g)[:, 0:n * DEN]).then_inc(s_wh_sb, 1)

            def columns(lo, hi):
                t = awh[:, lo:hi, D:DEN]
                nc.scalar.activation(a_col[:, lo:hi, None], t, ACT.Exp, bias=shift[:, 0:1]).then_inc(s_ac, 1)
                nc.scalar.activation(c_col[:, lo:hi, None], t, ACT.Exp, bias=shift[:, 1:2], scale=-(1.0 - SLOPE)).then_inc(s_ac, 1)

            def f_part(i, lo, hi):
                act.wait_ge(s_fcap[i], 1)
                nc.scalar.activation(f_row[:, lo:hi], f_row[:, lo:hi], ACT.Exp, bias=shift[:, 1:2], scale=1.0 - SLOPE).then_inc(s_f, 1)

            relu(NB, 1, TW)
            wh_copied(0, min(3, WHA))
            deviations(NB, TW)
            wh_copied(3, min(5, WHA))
            x1_copied(NB, TW)
            x1_stored(NB)
            wh_copied(5, min(7, WHA))
            scores_out(NB, TW)
            nc.scalar.activation(table_warm[:, :], eps_col[:, :], ACT.Exp)
            wh_copied(7, WHA)
            store_masks(NB, 1, TW)

            act.wait_ge(s_shift, 1)
            act.wait_ge(s_wh_sb, WHA)
            columns(0, 3 * WHA)
            f_part(0, 0, IB)
            for g in range(WHA, WHG):
                wh_copied(g, g + 1)
                act.wait_ge(s_wh_sb, g + 1)
                columns(3 * g, min(STEPS, 3 * g + 3))
            f_part(1, IB, NP)
            act.wait_ge(s_whm, 1)
            nc.scalar.copy(wh_mean[:, :], banks[4][:, 0:D]).then_inc(s_wm, 1)

            def copied_out(k, par, width):
                act.wait_ge(s_pu, STEPS * (k + 1))
                if not (isinstance(k, int) and k == 0):
                    act.wait_ge(s_num, 3 * k)
                for q in range(2):
                    m = min(2, len(tiles_of(width)) - 2 * q)
                    nc.scalar.copy(o_sb[:, 2 * q:2 * q + m, :],
                                   banks[2 * par + q][:, 0:m * DEN].rearrange("p (t d) -> p t d", d=DEN)).then_inc(s_ev, 1)

            def elu_exp(k, width):
                w = len(tiles_of(width)) * D
                act.wait_ge(s_h2, 2 * k + 2)
                nc.scalar.activation(el[:, 1, 0:w], el[:, 1, 0:w], ACT.Exp).then_inc(s_exp, 1)

            def stored(k, width):
                nt = len(tiles_of(width))
                act.wait_ge(s_mv, k + 1)
                if not (isinstance(k, int) and k == 0):
                    act.wait_ge(s_fin, k)
                nc.scalar.activation(std_o[:, 0:nt], mv[:, 0:nt, 1:2].rearrange("p t o -> p (t o)"), ACT.Sqrt,
                                     bias=eps_col[:, 0:1]).then_inc(s_rs, 1)
                act.wait_ge(s_fin, k + 1)
                if width == IB:
                    rows = out[bass.ds(k * IB, IB), :].rearrange("(t p) d -> p t d", p=P)
                    for t in (0, TPB // 2):
                        act.dma_start(rows[:, t:t + TPB // 2, :], o_out[:, t:t + TPB // 2, :]).then_inc(s_out, 16)
                else:
                    full = TAIL // P
                    act.dma_start(out[NB * IB:NB * IB + full * P, :].rearrange("(t p) d -> p t d", p=P), o_out[:, 0:full, :]).then_inc(s_out, 16)
                    act.dma_start(out[NB * IB + full * P:N, :], o_out[0:TAIL - full * P, full, :]).then_inc(s_out, 16)

            def layer2(k, par, width, first):
                copied_out(k, par, width)
                elu_exp(k, width)
                stored(k, width)

            blocks(act, layer2)
            act.wait_ge(s_out, 32 * (NB + 1))


_INS = ['x', 'adj', 'L0_gnn_item_feat', 'L0_gnn_W_item', 'L0_gnn_b_item', 'L0_gnn_W_user', 'L0_gnn_b_user', 'L1_gnn_W', 'L1_gnn_a']


def kernel(**inputs):
    import numpy as _np
    import concourse.bacc as _bacc
    from concourse import mybir as _mybir
    from concourse.bass_utils import run_bass_kernel_spmd as _run

    nc = _bacc.Bacc("TRN2", target_bir_lowering=False, num_devices=1)
    arrays, args = {}, []
    for name in _INS:
        a = _np.ascontiguousarray(inputs[name])
        arrays[f"in_{name}_dram"] = a
        args.append(nc.dram_tensor(f"in_{name}_dram", a.shape, _mybir.dt.from_np(a.dtype), kind="ExternalInput").ap())
    out = nc.dram_tensor("out_0_dram", inputs['x'].shape, _mybir.dt.float32, kind="ExternalOutput").ap()
    resnorm_two_graph_layers(nc, *args, out)
    r = _run(nc, [arrays], core_ids=[0])
    return r.results[0]["out_0_dram"]
```

```python
from contextlib import ExitStack

import concourse.bass as bass
from concourse import mybir

ALU = mybir.AluOpType
ACT = mybir.ActivationFunctionType
F32 = mybir.dt.float32
U8 = mybir.dt.uint8
U32 = mybir.dt.uint32
AX_X = mybir.AxisListType.X

P = 128
D = 128
Q = 32
A = P // Q
IB = 512
TPB = IB // P
GPB = IB // Q
JC = 1024
JA = JC // A
SPC = JA // Q
HG = GPB // 2
LN_EPS = 1e-5
SLOPE = 0.2
F_CAP = 75.0
BITS = 8


def resnorm_two_graph_layers(nc, x, adj, item, w_item, b_item, w_user, b_user, w_att, a_att, out):
    N = x.shape[0]
    NB = N // IB
    TAIL = N - NB * IB
    TG = -(-TAIL // Q)
    TW = TG * Q
    NC = N // JC + 1
    LJ = (N - (NC - 1) * JC) // A
    LS = -(-LJ // Q)
    LPAD = LS * Q - LJ
    STEPS = (NC - 1) * SPC + LS
    NP = NB * IB + IB
    RAW = 5 if (2 * NC) % 5 == 0 else 4
    LOFF = JA - LJ
    RAWW = JA + LPAD
    HC = NC // 2
    DEN = D + 1
    WHG = -(-STEPS // 3)
    WHA = min(13, (NC - 1) * SPC // 3)
    assert N % A == 0 and 0 < TAIL < IB and 0 <= LPAD < Q and 0 < LJ <= JA and NC % 2 == 0 and NC >= 4
    assert (2 * NC) % RAW == 0 and NB % 2 == 1 and TG > HG
    assert SPC * D == 2 * IB and SPC == BITS and IB == 2 * JA and NB - 1 == 2 * (NC - 1)

    def steps_of(c):
        return SPC if c < NC - 1 else LS

    def cols_of(c):
        return JA if c < NC - 1 else LJ

    with ExitStack() as ctx:
        def sb(name, shape, dt=F32):
            return ctx.enter_context(nc.sbuf_tensor(name, shape, dt))

        def sem(name):
            return ctx.enter_context(nc.semaphore(name))

        mask_dram = nc.dram_tensor("mask_scratch", [NB + 1, P, NC * IB], U8, kind="Internal").ap()
        x1_dram = nc.dram_tensor("x1_scratch", [NP, D], F32, kind="Internal").ap()
        s_dram = nc.dram_tensor("s_scratch", [1, NP], F32, kind="Internal").ap()

        area_h = sb("area_h", [P, STEPS * DEN])
        h = area_h[:, 0:STEPS * D].rearrange("p (s d) -> p s d", d=D)
        awh = area_h[:, :].rearrange("p (s d) -> p s d", d=DEN)
        raw_words = RAW * HG * RAWW
        t_words = 2 * SPC * IB
        area_1 = sb("area_1", [P, max(raw_words + t_words, NP + 3 * NC * IB // 4 + 8 * IB)])
        raw = area_1[:, 0:raw_words].rearrange("p (r g w) -> p r g w", r=RAW, g=HG)
        adj_t = area_1[:, raw_words:raw_words + t_words].rearrange("p (b w) -> p b w", b=2)
        f_row = area_1[:, 0:NP]
        taken = [NP]

        def behind_f(words):
            taken[0] += words
            return area_1[:, taken[0] - words:taken[0]]

        packed_in = behind_f(2 * NC * IB // 4).rearrange("p (b w) -> p b w", b=2)
        o_sb = behind_f(TPB * DEN).rearrange("p (t d) -> p t d", d=DEN)
        el = behind_f(3 * IB).rearrange("p (b w) -> p b w", b=3)
        x1_in = behind_f(IB).rearrange("p (t d) -> p t d", d=D)
        o_out = behind_f(IB).rearrange("p (t d) -> p t d", d=D)
        area_x = sb("area_x", [P, max(NP, 7 * JC)])
        x1_t = area_x[:, 0:NP]
        item_t = area_x[:, 0:2 * JC].rearrange("p (b w) -> p b w", b=2)
        item_in = area_x[:, 2 * JC:6 * JC].rearrange("p (b t d) -> p b t d", b=4, d=D)
        item_plain = area_x[:, 6 * JC:7 * JC]

        area_m = sb("area_m", [P, 2, SPC * IB // 4])
        mask_out = area_m.bitcast(U8)
        packing = sb("packing", [P, 6 * IB // 4], U32)
        packed = sb("packed", [P, 2, HC * IB // 4], U32)
        unpacked = sb("unpacked", [P, 2, SPC, IB // 4], U32)
        x1_plain = unpacked[:, 1, :, :].rearrange("p s w -> p (s w)").bitcast(F32)
        bit_of = sb("bit_of", [P, SPC], U32)
        bit_inv = sb("bit_inv", [P, STEPS])
        table_warm = sb("table_warm", [P, 1])
        ident = sb("ident", [P, P])
        ones = sb("ones", [P, P])
        w_in = sb("w_in", [P, 3, D])
        w_t = sb("w_t", [P, 3, D])
        a_cols = sb("a_cols", [P, 2])
        w_den = sb("w_den", [P, SPC, DEN])
        w_ts = sb("w_ts", [P, 2])
        b_item_row = sb("b_item_row", [P, D])
        b_user_col = sb("b_user_col", [P, 1])
        eps_col = sb("eps_col", [P, 1])
        area_s = sb("area_s", [P, SPC, IB])
        x_in = area_s[:, 0, :].rearrange("p (t d) -> p t d", d=D)
        x_t, yz, x1_blk = (area_s[:, i, :] for i in range(1, 4))
        x1_rows = area_s[:, 4, :].rearrange("p (t d) -> p t d", d=D)
        prob = area_s
        ts_col = sb("ts_col", [P, TPB, 2])
        t_max = sb("t_max", [P, NB + 1])
        t_part = sb("t_part", [P, 1])
        t_top = sb("t_top", [1, 1])
        shift = sb("shift", [P, 4])
        a_col = sb("a_col", [P, STEPS])
        c_col = sb("c_col", [P, STEPS])
        x_sums = sb("x_sums", [P, NB + 1])
        x_sum = sb("x_sum", [P, 1])
        x_mean = sb("x_mean", [P, P])
        wh_mean = sb("wh_mean", [P, D])
        den = sb("den", [P, 3, TPB])
        stats = sb("stats", [P, TPB, 6])
        mv = sb("mv", [P, TPB, 2])
        std_o = sb("std_o", [P, TPB])
        rstd_o = sb("rstd_o", [P, TPB])

        banks = [ctx.enter_context(nc.psum_tensor(f"bank{i}", [P, IB], F32)) for i in range(8)]
        ps_x, ps_z, ps_ts, ps_back, ps_top = banks[1:6]
        acc = (banks[0], banks[6])
        item_banks = (banks[4:6], banks[2:4])
        h_banks = (banks[0:2], banks[6:8])

        weights_loaded = sem("weights_loaded")
        constants_made = sem("constants_made")
        w_den_made = sem("w_den_made")
        weights_turned = sem("weights_turned")
        weights_turned_sb = sem("weights_turned_sb")
        wa_product = sem("wa_product")
        wa_sb = sem("wa_sb")
        item_loaded = [sem(f"item_loaded{i}") for i in range(4)]
        item_turned = sem("item_turned")
        item_turned_sb = sem("item_turned_sb")
        h_product = sem("h_product")
        h_ready = sem("h_ready")
        padding_cleared = sem("padding_cleared")
        adj_loaded = [sem(f"adj_loaded{i}") for i in range(RAW)]
        half_turned = sem("half_turned")
        chunk_contracted = sem("chunk_contracted")
        mask_made = sem("mask_made")
        packed_to_4 = sem("packed_to_4")
        packed_to_2 = sem("packed_to_2")
        packed_to_1 = sem("packed_to_1")
        masks_stored = [sem("masks_stored0"), sem("masks_stored1")]
        x_loaded = sem("x_loaded")
        x_turned = sem("x_turned")
        x_turned_sb = sem("x_turned_sb")
        relu_done = sem("relu_done")
        residual_added = sem("residual_added")
        z_rows_ready = sem("z_rows_ready")
        norm1_stats = sem("norm1_stats")
        norm1_moments = sem("norm1_moments")
        norm1_deviations = sem("norm1_deviations")
        norm1_reciprocals = sem("norm1_reciprocals")
        x1_rows_ready = sem("x1_rows_ready")
        x1_turned = sem("x1_turned")
        x1_turned_sb = sem("x1_turned_sb")
        x1_kept = sem("x1_kept")
        scores_product = sem("scores_product")
        scores_sb = sem("scores_sb")
        t_max_taken = sem("t_max_taken")
        x1_stored_dram = sem("x1_stored_dram")
        s_stored_dram = sem("s_stored_dram")
        top_partial = sem("top_partial")
        top_turned = sem("top_turned")
        top_found = sem("top_found")
        top_broadcast = sem("top_broadcast")
        shifts_made = sem("shifts_made")
        x1_plain_made = sem("x1_plain_made")
        last_chunk_ordered = sem("last_chunk_ordered")
        item_plain_made = sem("item_plain_made")
        wh_product = sem("wh_product")
        wh_sb = sem("wh_sb")
        columns_made = sem("columns_made")
        right_ready = sem("right_ready")
        s_loaded = [sem("s_loaded0"), sem("s_loaded1")]
        s_capped = [sem("s_capped0"), sem("s_capped1")]
        f_ready = sem("f_ready")
        x1_summed = sem("x1_summed")
        x1_mean_made = sem("x1_mean_made")
        wh_mean_product = sem("wh_mean_product")
        wh_mean_ready = sem("wh_mean_ready")
        mask_loaded = [sem("mask_loaded0"), sem("mask_loaded1")]
        mask_unpacked = sem("mask_unpacked")
        weights_made = sem("weights_made")
        step_contracted = sem("step_contracted")
        sums_sb = sem("sums_sb")
        denominator_steps = sem("denominator_steps")
        quotient_steps = sem("quotient_steps")
        elu_halves = sem("elu_halves")
        elu_exp_done = sem("elu_exp_done")
        elu_done = sem("elu_done")
        x1_loaded = sem("x1_loaded")
        residual2_added = sem("residual2_added")
        norm2_stats = sem("norm2_stats")
        norm2_moments = sem("norm2_moments")
        norm2_deviations = sem("norm2_deviations")
        norm2_reciprocals = sem("norm2_reciprocals")
        rows_ready = sem("rows_ready")
        rows_stored = sem("rows_stored")

        block = ctx.enter_context(nc.Block())

        def blocks(eng, body):
            body(0, 0, IB, True)
            body(1, 1, IB, False)
            body(2, 0, IB, False)
            with eng.Fori(3, NB - 1, 2) as k:
                body(k, 1, IB, False)
                body(k + 1, 0, IB, False)
            body(NB, 1, TW, False)

        def at(c):
            return min(c, NC - 1)

        def in_step_order(copy, dst, src, last_chunk):
            if not last_chunk:
                return [copy(dst.rearrange("p (s a j) -> p a s j", a=A, j=Q), src.rearrange("p (a s j) -> p a s j", a=A, j=Q))]
            whole = LJ // Q
            one = copy(dst[:, 0:whole * P].rearrange("p (s a j) -> p a s j", a=A, j=Q),
                       src[:, 0:A * LJ].rearrange("p (a w) -> p a w", a=A)[:, :, 0:whole * Q].rearrange("p a (s j) -> p a s j", j=Q))
            two = copy(dst[:, whole * P:(whole + 1) * P].rearrange("p (a j) -> p a j", a=A),
                       src[:, whole * Q:whole * Q + A * LJ].rearrange("p (a w) -> p a w", a=A)[:, :, 0:Q])
            return [one, two]

        def wh_bank(g):
            return (banks[7], banks[0], banks[1])[g % 3] if g < WHA else banks[4 + (g - WHA) % 4]

        def tiles_of(width):
            return [(t, min(P, width - t * P)) for t in range(-(-width // P))]

        def epilogue(eng, ops, k, width, first):
            nt = len(tiles_of(width))
            w = nt * D
            num = o_sb[:, 0:nt, 0:D]
            e0, e1, e2 = (el[:, i, 0:w].rearrange("p (t d) -> p t d", d=D) for i in range(3))
            if first:
                eng.wait_ge(wh_mean_ready, 1)
            eng.wait_ge(denominator_steps, 3 * (k + 1))
            ops.tensor_tensor(e0, wh_mean[:, None, :].to_broadcast([P, nt, D]),
                              den[:, 0, 0:nt, None].to_broadcast([P, nt, D]), ALU.mult).then_inc(quotient_steps, 1)
            eng.wait_ge(quotient_steps, 3 * k + 1)
            ops.tensor_tensor(e1, e0, num, ALU.add).then_inc(quotient_steps, 1)
            eng.wait_ge(quotient_steps, 3 * k + 2)
            ops.tensor_tensor(e0, e1, den[:, 2, 0:nt, None].to_broadcast([P, nt, D]), ALU.mult).then_inc(quotient_steps, 1)
            eng.wait_ge(quotient_steps, 3 * k + 3)
            ops.nop(nofuse=True)
            ops.tensor_scalar(el[:, 1, 0:w], el[:, 0, 0:w], 0.0, None, ALU.min).then_inc(elu_halves, 1)
            if not (isinstance(k, int) and k == 0):
                eng.wait_ge(rows_ready, k)
                ops.nop(nofuse=True)
            ops.tensor_scalar(el[:, 2, 0:w], el[:, 0, 0:w], 0.0, -1.0, ALU.max, ALU.add).then_inc(elu_halves, 1)
            eng.wait_ge(elu_exp_done, k + 1)
            eng.wait_ge(elu_halves, 2 * k + 2)
            ops.tensor_tensor(el[:, 0, 0:w], el[:, 1, 0:w], el[:, 2, 0:w], ALU.add).then_inc(elu_done, 1)
            eng.wait_ge(elu_done, k + 1)
            eng.wait_ge(x1_loaded, 16 * (k + 1))
            ops.tensor_tensor(e2, e0, x1_in[:, 0:nt, :], ALU.add).then_inc(residual2_added, 1)

        @block.sync
        def _(sp):
            def load_item(c):
                if c >= 4:
                    sp.wait_ge(item_turned, c - 3)
                lo, hi = c * JC, min(N, (c + 1) * JC)
                full = (hi - lo) // P
                sp.dma_start(item_in[:, c % 4, 0:full, :], item[lo:lo + full * P, :].rearrange("(t p) d -> p t d", p=P)).then_inc(item_loaded[c % 4], 16)
                if hi - lo > full * P:
                    sp.dma_start(item_in[0:hi - lo - full * P, c % 4, full, :], item[lo + full * P:hi, :]).then_inc(item_loaded[c % 4], 16)

            load_item(0)
            for n, w in enumerate((w_item, w_user, w_att)):
                sp.dma_start(w_in[:, n, :], w).then_inc(weights_loaded, 16)
            sp.dma_start(a_cols[:, 0:1], a_att[0:D, :]).then_inc(weights_loaded, 16)
            sp.dma_start(a_cols[:, 1:2], a_att[D:2 * D, :]).then_inc(weights_loaded, 16)
            sp.dma_start(b_item_row[:, :], b_item.rearrange("(a d) -> a d", a=1).to_broadcast([P, D])).then_inc(weights_loaded, 16)
            sp.dma_start(b_user_col[:, :], b_user.rearrange("(d a) -> d a", a=1)).then_inc(weights_loaded, 16)
            for c in range(1, 4):
                load_item(c)

            def load_half(k, n, width):
                c, half = n // 2, n % 2
                slot = n % RAW
                groups = HG if half == 0 or width == IB else width // Q - HG
                rows = Q if half == 0 or width == IB else TAIL - HG * Q - (groups - 1) * Q
                off = 0 if c < NC - 1 else LOFF
                if not (isinstance(k, int) and k * 2 * NC + n < RAW):
                    sp.wait_ge(half_turned, k * (2 * NC) + n - RAW + 1)
                for a in (0, 2, 1, 3):
                    cols = slice(c * JC + a * cols_of(c), c * JC + (a + 1) * cols_of(c))
                    if rows == Q:
                        src = adj[bass.ds(k * IB + half * HG * Q, groups * Q), cols].rearrange("(g i) w -> i g w", i=Q)
                        dst = raw[a * Q:(a + 1) * Q, slot, 0:groups, off:off + cols_of(c)]
                    else:
                        assert groups == 1
                        src = adj[N - rows:N, cols]
                        dst = raw[a * Q:a * Q + rows, slot, 0, off:off + cols_of(c)]
                    sp.dma_start(dst, src).then_inc(adj_loaded[slot], 16)

            def load_x(k, width):
                if not (isinstance(k, int) and k == 0):
                    sp.wait_ge(x_turned, k)
                if width == IB:
                    rows = x[bass.ds(k * IB, IB), :].rearrange("(t p) d -> p t d", p=P)
                    for t in (0, TPB // 2):
                        sp.dma_start(x_in[:, t:t + TPB // 2, :], rows[:, t:t + TPB // 2, :]).then_inc(x_loaded, 16)
                else:
                    full = TAIL // P
                    sp.dma_start(x_in[:, 0:full, :], x[NB * IB:NB * IB + full * P, :].rearrange("(t p) d -> p t d", p=P)).then_inc(x_loaded, 16)
                    sp.dma_start(x_in[0:TAIL - full * P, full, :], x[NB * IB + full * P:N, :]).then_inc(x_loaded, 16)

            def block_loads(k, par, width, first):
                for n in range(2 * NC):
                    if first and n < RAW:
                        continue
                    if n == 0:
                        load_x(k, width)
                    load_half(k, n, width)

            load_x(0, IB)
            for c in range(4, NC):
                load_item(c)
                if c % 2 == 1:
                    load_half(0, (c - 5) // 2, IB)
            for n in range(NC // 2 - 2, RAW):
                load_half(0, n, IB)
            blocks(sp, block_loads)

            def load_mask(k, par, width):
                sp.dma_start(packed_in[:, par, 0:NC * width // 4],
                             mask_dram[bass.ds(k, 1), :, 0:NC * width].rearrange("o p w -> (o p) w").bitcast(F32)).then_inc(mask_loaded[par], 16)

            def load_x1(k):
                if not (isinstance(k, int) and k == 0):
                    sp.wait_ge(residual2_added, k)
                sp.dma_start(x1_in[:, :, :], x1_dram[bass.ds(k * IB, IB), :].rearrange("(t p) d -> p t d", p=P)).then_inc(x1_loaded, 16)

            def next_mask(k, par, width):
                sp.wait_ge(mask_unpacked, k * NC)
                load_mask(k + 1, 1 - par, width)

            sp.wait_ge(half_turned, 2 * NC * (NB + 1))
            sp.wait_ge(chunk_contracted, NC * (NB + 1))
            sp.wait_ge(mask_made, NC * (NB + 1))
            sp.wait_ge(s_stored_dram, 16 * NB)
            sp.dma_start(f_row[:, 0:IB], s_dram[:, 0:IB].to_broadcast([P, IB])).then_inc(s_loaded[0], 16)
            load_mask(0, 0, IB)
            sp.wait_ge(s_stored_dram, 16 * (NB + 1))
            sp.dma_start(f_row[:, IB:NP], s_dram[:, IB:NP].to_broadcast([P, NP - IB])).then_inc(s_loaded[1], 16)
            sp.wait_ge(x1_stored_dram, 16 * (NB + 1))
            load_x1(0)
            sp.wait_ge(masks_stored[0], 16 * (NB + 1))
            sp.wait_ge(masks_stored[1], 16 * (NB + 1))
            load_mask(1, 1, IB)
            next_mask(1, 1, IB)
            load_x1(1)
            next_mask(2, 0, IB)
            load_x1(2)
            with sp.Fori(3, NB - 3, 2) as k:
                next_mask(k, 1, IB)
                load_x1(k)
                next_mask(k + 1, 0, IB)
                load_x1(k + 1)
            next_mask(NB - 2, 1, IB)
            load_x1(NB - 2)
            next_mask(NB - 1, 0, TW)
            load_x1(NB - 1)
            load_x1(NB)

        @block.gpsimd
        def _(pool):
            nc.gpsimd.memset(ones[:, :], 1.0).then_inc(constants_made, 1)
            nc.gpsimd.memset(ident[:, :], 0.0).then_inc(constants_made, 1)
            pool.wait_ge(constants_made, 2)
            nc.gpsimd.affine_select(out=ident[:, :], in_=ident[:, :], compare_op=ALU.not_equal, fill=1.0, base=0,
                                    pattern=[[-1, P]], channel_multiplier=1).then_inc(constants_made, 1)
            for n in range(SPC):
                bit = 1 << (SPC - 1 - n)
                nc.gpsimd.memset(bit_of.bitcast(U8)[:, 4 * n:4 * n + 4], bit)
                last = nc.gpsimd.memset(bit_inv[:, n:STEPS:SPC], 1.0 / bit)
            last.then_inc(constants_made, 1)
            nc.gpsimd.memset(item_plain[:, :], 0.0).then_inc(constants_made, 1)
            nc.gpsimd.memset(eps_col[:, :], LN_EPS).then_inc(constants_made, 1)
            for n in (2 * NC - 2, 2 * NC - 1):
                nc.gpsimd.memset(raw[:, n % RAW, :, JA:RAWW], 0.0).then_inc(padding_cleared, 1)

            last_chunk = x1_t[:, (NC - 1) * JC:NC * JC]

            def keep_x1(k, par, width, first):
                if width == IB:
                    chunk = x1_t[:, bass.ds((k - par) * IB, JC)].rearrange("p (s a j) -> p a s j", a=A, j=Q)
                    pool.wait_ge(x1_turned_sb, k + 1)
                    nc.gpsimd.tensor_copy(chunk[:, 2 * par:2 * par + 2, :, :],
                                          x1_blk.rearrange("p (a s j) -> p a s j", a=2, j=Q)).then_inc(x1_kept, 1)
                else:
                    pool.wait_ge(x1_kept, NB)
                    nc.gpsimd.tensor_copy(x1_plain[:, 0:IB].rearrange("p (a s j) -> p a s j", a=2, j=Q),
                                          last_chunk.rearrange("p (s a j) -> p a s j", a=A, j=Q)[:, 0:2, :, :]).then_inc(x1_plain_made, 1)
                    nc.gpsimd.memset(x1_plain[:, IB + TW:IB + TW + Q], 0.0).then_inc(x1_plain_made, 1)
                    pool.wait_ge(x1_turned_sb, k + 1)
                    nc.gpsimd.tensor_copy(x1_plain[:, IB:IB + width], x1_blk[:, 0:width]).then_inc(x1_kept, 1)

            blocks(pool, keep_x1)
            pool.wait_ge(x1_plain_made, 2)
            pool.wait_ge(x1_kept, NB + 1)
            in_step_order(nc.gpsimd.tensor_copy, last_chunk[:, 0:LS * P], x1_plain, True)[-1].then_inc(last_chunk_ordered, 1)

            pool.wait_ge(shifts_made, 1)
            pool.wait_ge(s_loaded[1], 16)
            nc.gpsimd.tensor_scalar(f_row[:, IB:NP], f_row[:, IB:NP], shift[:, 2:3], None, ALU.min).then_inc(s_capped[1], 1)
            pool.wait_ge(x1_summed, NB + 2)
            nc.gpsimd.tensor_scalar(x_mean[:, :], ones[:, :], x_sum[:, 0:1], 1.0 / N, ALU.mult, ALU.mult).then_inc(x1_mean_made, 1)

            def layer2(k, par, width, first):
                if not (isinstance(k, int) and k == NB):
                    epilogue(pool, nc.gpsimd, k, width, first)

            blocks(pool, layer2)

        @block.tensor
        def _(pe):
            def item_transposes(c):
                n = min(N, (c + 1) * JC) - c * JC
                pe.wait_ge(item_loaded[c % 4], 16 * (c // 4 + 1) if c < NC - 1 else 16 * (c // 4 + 2))
                if c == 1:
                    pe.wait_ge(wa_sb, 1)
                if c >= 2:
                    pe.wait_ge(item_turned_sb, c - 1)
                for t in range(-(-n // P)):
                    m = min(P, n - t * P)
                    mm = nc.tensor.transpose(item_banks[c % 2][t // 4][:, (t % 4) * P:(t % 4) * P + m],
                                             item_in[0:m, c % 4, t, :], ident[0:m, 0:m])
                mm.then_inc(item_turned, 1)

            def h_products(c):
                pe.wait_ge(item_turned_sb, c + 1)
                if c >= 2:
                    pe.wait_ge(h_ready, c - 1)
                for s in range(steps_of(c)):
                    mm = nc.tensor.matmul(h_banks[c % 2][s // 4][:, (s % 4) * D:(s % 4 + 1) * D],
                                          item_t[:, c % 2, s * P:(s + 1) * P], w_t[:, 0, :], start=True, stop=True)
                mm.then_inc(h_product, 1)

            pe.wait_ge(constants_made, 3)
            item_transposes(0)
            pe.wait_ge(weights_loaded, 16 * 7)
            for n in range(3):
                mm = nc.tensor.transpose(banks[n][:, 0:D], w_in[:, n, :], ident[:, :])
            mm.then_inc(weights_turned, 1)
            pe.wait_ge(weights_turned_sb, 1)
            nc.tensor.matmul(banks[3][:, 0:1], w_t[:, 2, :], a_cols[:, 1:2], start=True, stop=True)
            nc.tensor.matmul(banks[3][:, 1:2], w_t[:, 2, :], a_cols[:, 0:1], start=True, stop=True).then_inc(wa_product, 1)
            for c in range(NC):
                if c + 1 < NC:
                    item_transposes(c + 1)
                h_products(c)

            def z_rows(k, width):
                pe.wait_ge(residual_added, k + 1)
                if not (isinstance(k, int) and k == 0):
                    pe.wait_ge(x1_rows_ready, k)
                for t, m in tiles_of(width):
                    mm = nc.tensor.transpose(ps_z[0:m, t * P:t * P + D], yz[:, t * P:t * P + m], ident[:, :])
                mm.then_inc(z_rows_ready, 1)

            def x1_back(k, width):
                pe.wait_ge(x1_rows_ready, k + 1)
                if not (isinstance(k, int) and k == 0):
                    pe.wait_ge(x1_turned_sb, k)
                for t, m in tiles_of(width):
                    mm = nc.tensor.transpose(ps_back[:, t * P:t * P + m], x1_rows[0:m, t, :], ident[0:m, 0:m])
                mm.then_inc(x1_turned, 1)

            def score_parts(k, width):
                pe.wait_ge(x1_turned_sb, k + 1)
                if not (isinstance(k, int) and k == 0):
                    pe.wait_ge(scores_sb, k)
                for t, m in tiles_of(width):
                    mm = nc.tensor.matmul(ps_ts[0:m, 2 * t:2 * t + 2], x1_blk[:, t * P:t * P + m], w_ts[:, :], start=True, stop=True)
                mm.then_inc(scores_product, 1)

            def contract(k, par, width, first):
                pe.wait_ge(x_loaded, 32 * (k + 1))
                if not first:
                    pe.wait_ge(x_turned_sb, k)
                live = tiles_of(width) if width == IB else tiles_of(TAIL)
                for t, m in live:
                    mm = nc.tensor.transpose(ps_x[:, t * P:t * P + m], x_in[0:m, t, :], ident[0:m, 0:m])
                mm.then_inc(x_turned, 1)
                for c in range(NC):
                    if first and c == 1:
                        pe.wait_ge(h_ready, NC)
                    pe.wait_ge(half_turned, k * (2 * NC) + 2 * c + 2)
                    if c == 0 and not (isinstance(k, int) and k < 2):
                        pe.wait_ge(relu_done, k - 1)
                    if c == at(4):
                        pe.wait_ge(x_turned_sb, k + 1)
                        nc.tensor.matmul(acc[par][:, 0:width], w_t[:, 1, :], x_t[:, 0:width], start=False, stop=False)
                    for s in range(steps_of(c)):
                        mm = nc.tensor.matmul(acc[par][:, 0:width], h[:, c * SPC + s, :],
                                              adj_t[:, c % 2, s * width:(s + 1) * width],
                                              start=(c == 0 and s == 0), stop=(c == NC - 1 and s == LS - 1))
                    mm.then_inc(chunk_contracted, 1)
                    if not first:
                        if c == 1:
                            z_rows(k - 1, IB)
                        if c == at(4):
                            x1_back(k - 1, IB)
                        if c == at(5):
                            score_parts(k - 1, IB)

            pe.wait_ge(h_ready, NC - 1)
            blocks(pe, contract)

            def wh_products(g):
                before = [f for f in range(g) if wh_bank(f) is wh_bank(g)]
                if before:
                    pe.wait_ge(wh_sb, before[-1] + 1)
                for b in range(3 * g, min(STEPS, 3 * g + 3)):
                    if b == (NC - 1) * SPC:
                        pe.wait_ge(last_chunk_ordered, 1)
                    mm = nc.tensor.matmul(wh_bank(g)[:, (b - 3 * g) * DEN:(b - 3 * g + 1) * DEN],
                                          x1_t[:, b * P:(b + 1) * P], w_den[:, b % SPC, :], start=True, stop=True)
                mm.then_inc(wh_product, 1)

            def some_wh(lo, hi):
                for g in range(lo, min(hi, WHA)):
                    wh_products(g)

            pe.wait_ge(x1_kept, NB - 1)
            pe.wait_ge(relu_done, NB)
            pe.wait_ge(w_den_made, 1)
            some_wh(0, 2)
            z_rows(NB, TW)
            some_wh(2, 5)
            x1_back(NB, TW)
            some_wh(5, 7)
            score_parts(NB, TW)
            some_wh(7, 10)
            pe.wait_ge(top_partial, 1)
            nc.tensor.transpose(ps_top[0:1, 0:P], t_part[:, :], ident[:, :]).then_inc(top_turned, 1)
            some_wh(10, 11)
            pe.wait_ge(top_found, 1)
            nc.tensor.matmul(ps_top[:, P:P + 1], ones[0:1, :], t_top[0:1, 0:1], start=True, stop=True).then_inc(top_broadcast, 1)
            some_wh(11, WHA)
            pe.wait_ge(x1_turned_sb, NB + 1)
            pe.wait_ge(shifts_made, 1)
            pe.wait_ge(wh_sb, WHA)

            def weighted(par, width, right, slot, start, stop):
                for t, m in tiles_of(width):
                    bank = banks[2 * par + t // 2]
                    mm = nc.tensor.matmul(bank[0:m, (t % 2) * DEN:(t % 2 + 1) * DEN], prob[:, slot, t * P:t * P + m],
                                          right, start=start and t % 2 == 0, stop=stop, skip_group_check=True)
                mm.then_inc(step_contracted, 1)

            def layer2(k, par, width, first):
                if not (isinstance(k, int) and k < 2):
                    pe.wait_ge(sums_sb, 2 * (k - 1))
                def chunk(c, first_block=False):
                    for n in range(steps_of(c) if isinstance(c, int) else SPC):
                        b = c * SPC + n
                        if first_block and b % 3 == 0 and WHA <= b // 3 + 3 < WHG:
                            wh_products(b // 3 + 3)
                        if first_block:
                            pe.wait_ge(right_ready, b // 3 + 1)
                        pe.wait_ge(weights_made, k * STEPS + b + 1)
                        if isinstance(c, int):
                            right = awh[:, b, :]
                        else:
                            right = area_h[:, bass.ds(c * (SPC * DEN) + n * DEN, DEN)]
                        weighted(par, width, right, n, isinstance(b, int) and b == 0, isinstance(b, int) and b == STEPS - 1)

                if first:
                    for c in range(NC):
                        chunk(c, True)
                    pe.wait_ge(x1_mean_made, 1)
                    nc.tensor.matmul(banks[4][:, 0:D], x_mean[:, :], w_in[:, 2, :], start=True, stop=True).then_inc(wh_mean_product, 1)
                    return
                chunk(0)
                with pe.Fori(1, NC - 1) as c:
                    chunk(c)
                chunk(NC - 1)

            blocks(pe, layer2)

        @block.vector
        def _(dve):
            dve.wait_ge(weights_turned, 1)
            for n in range(3):
                last = nc.vector.tensor_copy(w_t[:, n, :], banks[n][:, 0:D])
            last.then_inc(weights_turned_sb, 1)
            dve.wait_ge(wa_product, 1)
            nc.vector.tensor_copy(w_ts[:, :], banks[3][:, 0:2]).then_inc(wa_sb, 1)

            def half_transposed(k, n, width):
                c, half, slot = n // 2, n % 2, n % RAW
                steps = steps_of(c)
                groups = HG if half == 0 or width == IB else width // Q - HG
                off = 0 if c < NC - 1 else LOFF
                uses = k * (2 * NC // RAW) + n // RAW + 1
                dve.wait_ge(adj_loaded[slot], uses * (16 * A))
                if half == 0 and not (isinstance(k, int) and k * NC + c < 2):
                    dve.wait_ge(chunk_contracted, k * NC + c - 1)
                    dve.wait_ge(mask_made, k * NC + c - 1)
                g0 = half * HG
                dst = adj_t[:, c % 2, 0:steps * width].rearrange("p (s g i) -> p s g i", s=steps, i=Q)[:, :, g0:g0 + groups, :]
                src = raw[:, slot, 0:groups, off:off + steps * Q].rearrange("p g (s i) -> p s g i", i=Q)
                nc.vector.transpose(dst, src).then_inc(half_turned, 1)

            def residual(k, width):
                dve.wait_ge(relu_done, k + 1)
                nc.vector.tensor_tensor(yz[:, 0:width], yz[:, 0:width], x_t[:, 0:width], ALU.add).then_inc(residual_added, 1)

            def row_stats1(k, width):
                dve.wait_ge(z_rows_ready, k + 1)
                tiles = tiles_of(width)
                for t, m in tiles:
                    last = nc.vector.bn_stats(stats[0:m, t, :], ps_z[0:m, t * P:t * P + D])
                last.then_inc(norm1_stats, 1)
                dve.wait_ge(norm1_stats, k + 1)
                nc.vector.nop(nofuse=True)
                for t, m in tiles:
                    last = nc.vector.bn_aggr(mv[0:m, t, :], stats[0:m, t, :])
                last.then_inc(norm1_moments, 1)

            def normed(k, width):
                dve.wait_ge(norm1_deviations, k + 1)
                tiles = tiles_of(width)
                nc.vector.reciprocal(rstd_o[:, 0:len(tiles)], std_o[:, 0:len(tiles)]).then_inc(norm1_reciprocals, 1)
                dve.wait_ge(norm1_reciprocals, k + 1)
                if not (isinstance(k, int) and k == 0):
                    dve.wait_ge(x1_turned, k)
                    dve.wait_ge(x1_stored_dram, 16 * k)
                for t, m in tiles:
                    last = nc.vector.tensor_scalar(x1_rows[0:m, t, :], ps_z[0:m, t * P:t * P + D], mv[0:m, t, 0:1],
                                                   rstd_o[0:m, t:t + 1], ALU.subtract, ALU.mult)
                last.then_inc(x1_rows_ready, 1)

            def block_sums(k, width):
                dve.wait_ge(scores_sb, k + 1)
                nc.vector.reduce_max(t_max[:, bass.ds(k, 1)], ts_col[:, 0:len(tiles_of(width)), 0], AX_X).then_inc(t_max_taken, 1)
                live = width if width == IB else TAIL
                nc.vector.reduce_sum(x_sums[:, bass.ds(k, 1)], x1_blk[:, 0:live], AX_X).then_inc(x1_summed, 1)

            packs = packing[:, :].rearrange("p (s w) -> p s w", w=IB // 4)

            def pack1(k, c, width):
                dve.wait_ge(mask_made, k * NC + c + 1)
                w = width // 4
                m = mask_out[:, c % 2, 0:SPC * width].bitcast(U32).rearrange("p (s w) -> p s w", s=SPC)
                nc.vector.scalar_tensor_tensor(out=packs[:, 0:4, 0:w], in0=m[:, 0:4, :], scalar=4, in1=m[:, 4:8, :],
                                               op0=ALU.logical_shift_left, op1=ALU.bitwise_or).then_inc(packed_to_4, 1)

            def pack2(k, c, width):
                dve.wait_ge(packed_to_4, k * NC + c + 1)
                w = width // 4
                nc.vector.scalar_tensor_tensor(out=packs[:, 4:6, 0:w], in0=packs[:, 0:2, 0:w], scalar=2, in1=packs[:, 2:4, 0:w],
                                               op0=ALU.logical_shift_left, op1=ALU.bitwise_or).then_inc(packed_to_2, 1)

            def pack3(k, c, width):
                dve.wait_ge(packed_to_2, k * NC + c + 1)
                if c % HC == 0 and not (isinstance(k, int) and k == 0):
                    dve.wait_ge(masks_stored[c // HC], 16 * k)
                w = width // 4
                nc.vector.scalar_tensor_tensor(out=packed[:, c // HC, (c % HC) * w:(c % HC + 1) * w], in0=packs[:, 4, 0:w], scalar=1,
                                               in1=packs[:, 5, 0:w], op0=ALU.logical_shift_left, op1=ALU.bitwise_or).then_inc(packed_to_1, 1)

            EARLY = (NC - 3, NC - 1)
            for c in range(NC):
                if c == 1:
                    dve.wait_ge(constants_made, 4)
                    dve.wait_ge(wa_sb, 1)
                    for n in range(SPC):
                        nc.vector.tensor_scalar(w_den[:, n, 0:D], w_in[:, 2, :], bit_inv[:, n:n + 1], None, ALU.mult)
                        last = nc.vector.tensor_copy(w_den[:, n, D:DEN], w_ts[:, 0:1])
                    last.then_inc(w_den_made, 1)
                if c in EARLY:
                    half_transposed(0, EARLY.index(c), IB)
                n = steps_of(c)
                dve.wait_ge(h_product, c + 1)
                for q in range(-(-n // 4)):
                    m = min(4, n - 4 * q)
                    last = nc.vector.tensor_tensor(h[:, c * SPC + 4 * q:c * SPC + 4 * q + m, :],
                                                   h_banks[c % 2][q][:, 0:m * D].rearrange("p (s d) -> p s d", d=D),
                                                   b_item_row[:, None, :].to_broadcast([P, m, D]), ALU.add)
                last.then_inc(h_ready, 1)

            dve.wait_ge(padding_cleared, 2)

            def transposes(k, par, width, first):
                for c in range(NC):
                    one = (k, c - 1, width) if c >= 1 else (k - 1, NC - 1, IB)
                    two = (k, c - 2, width) if c >= 2 else (k - 1, NC + c - 2, IB)
                    if not first or 2 * c >= len(EARLY):
                        half_transposed(k, 2 * c, width)
                    if not first or c >= 2:
                        pack2(*two)
                    if not first or 2 * c + 1 >= len(EARLY):
                        half_transposed(k, 2 * c + 1, width)
                    if not first or c >= 2:
                        pack3(*two)
                    if not first or c >= 1:
                        pack1(*one)
                    if not first:
                        if c == 2:
                            residual(k - 1, IB)
                        if c == at(3):
                            row_stats1(k - 1, IB)
                        if c == at(4):
                            normed(k - 1, IB)
                        if c == NC - 1:
                            block_sums(k - 1, IB)

            blocks(dve, transposes)
            residual(NB, TW)
            row_stats1(NB, TW)
            normed(NB, TW)
            block_sums(NB, TW)

            dve.wait_ge(t_max_taken, NB + 1)
            nc.vector.reduce_max(t_part[:, :], t_max[:, :], AX_X).then_inc(top_partial, 1)
            pack2(NB, NC - 2, TW)
            pack3(NB, NC - 2, TW)
            pack1(NB, NC - 1, TW)
            dve.wait_ge(top_turned, 1)
            nc.vector.reduce_max(t_top[:, :], ps_top[0:1, 0:P], AX_X).then_inc(top_found, 1)
            pack2(NB, NC - 1, TW)
            pack3(NB, NC - 1, TW)
            dve.wait_ge(top_broadcast, 1)
            top = ps_top[:, P:P + 1]
            nc.vector.tensor_scalar(shift[:, 0:1], top, -1.0, None, ALU.mult)
            nc.vector.tensor_scalar(shift[:, 1:2], top, 1.0 - SLOPE, None, ALU.mult)
            nc.vector.tensor_scalar(shift[:, 2:3], top, -1.0, F_CAP / (1.0 - SLOPE), ALU.mult, ALU.add).then_inc(shifts_made, 1)
            dve.wait_ge(s_loaded[0], 16)
            dve.wait_ge(shifts_made, 1)
            nc.vector.tensor_scalar(f_row[:, 0:IB], f_row[:, 0:IB], shift[:, 2:3], None, ALU.min).then_inc(s_capped[0], 1)
            dve.wait_ge(x1_summed, NB + 1)
            nc.vector.reduce_sum(x_sum[:, :], x_sums[:, :], AX_X).then_inc(x1_summed, 1)

            def right_factor(g):
                n = min(STEPS, 3 * g + 3) - 3 * g
                dve.wait_ge(columns_made, 2 * (max(0, g - WHA + 1) + 1))
                mine = awh[:, 3 * g:3 * g + n, 0:D]
                a = a_col[:, 3 * g:3 * g + n, None]
                nc.vector.tensor_tensor(mine, mine, a.to_broadcast([P, n, D]), ALU.mult)
                nc.vector.tensor_tensor(awh[:, 3 * g:3 * g + n, D:DEN], a, bit_inv[:, 3 * g:3 * g + n, None], ALU.mult).then_inc(right_ready, 1)

            def weights(k, par, width, scalar, mask, slot):
                if isinstance(k, int):
                    lhs = f_row[:, k * IB:k * IB + width]
                else:
                    lhs = f_row[:, bass.ds(k * IB, width)]
                nc.vector.scalar_tensor_tensor(out=prob[:, slot, 0:width], in0=lhs, scalar=scalar, in1=mask,
                                               op0=ALU.max, op1=ALU.mult).then_inc(weights_made, 1)

            def denominators(k, width):
                nt = len(tiles_of(width))
                dve.wait_ge(sums_sb, 2 * (k + 1))
                if not (isinstance(k, int) and k == 0):
                    dve.wait_ge(quotient_steps, 3 * k)
                d_in = o_sb[:, 0:nt, D:DEN].rearrange("p t o -> p (t o)")
                nc.vector.tensor_scalar(den[:, 0, 0:nt], d_in, 0.0, None, ALU.is_equal).then_inc(denominator_steps, 1)
                dve.wait_ge(denominator_steps, 3 * k + 1)
                nc.vector.tensor_tensor(den[:, 1, 0:nt], den[:, 0, 0:nt], d_in, ALU.add).then_inc(denominator_steps, 1)
                dve.wait_ge(denominator_steps, 3 * k + 2)
                nc.vector.reciprocal(den[:, 2, 0:nt], den[:, 1, 0:nt]).then_inc(denominator_steps, 1)

            def row_stats(k, width):
                nt = len(tiles_of(width))
                dve.wait_ge(residual2_added, k + 1)
                z = el[:, 2, 0:nt * D].rearrange("p (t d) -> p t d", d=D)
                for t in range(nt):
                    last = nc.vector.bn_stats(stats[:, t, :], z[:, t, :])
                last.then_inc(norm2_stats, 1)
                dve.wait_ge(norm2_stats, k + 1)
                nc.vector.nop(nofuse=True)
                for t in range(nt):
                    last = nc.vector.bn_aggr(mv[:, t, :], stats[:, t, :])
                last.then_inc(norm2_moments, 1)

            def scaled(k, width):
                nt = len(tiles_of(width))
                z = el[:, 2, 0:nt * D].rearrange("p (t d) -> p t d", d=D)
                dve.wait_ge(norm2_deviations, k + 1)
                nc.vector.reciprocal(rstd_o[:, 0:nt], std_o[:, 0:nt]).then_inc(norm2_reciprocals, 1)
                dve.wait_ge(norm2_reciprocals, k + 1)
                if not (isinstance(k, int) and k == 0):
                    dve.wait_ge(rows_stored, 32 * k)
                for t in range(nt):
                    last = nc.vector.tensor_scalar(o_out[:, t, :], z[:, t, :], mv[:, t, 0:1], rstd_o[:, t:t + 1],
                                                   ALU.subtract, ALU.mult)
                last.then_inc(rows_ready, 1)

            def unpack(k, par, width, c, slot):
                w = width // 4
                if isinstance(c, int):
                    if c == 0:
                        dve.wait_ge(mask_loaded[par], (k + 1) * 8 if par == 1 else (k + 2) * 8)
                    if not (isinstance(k, int) and k == 0 and c < 2):
                        dve.wait_ge(weights_made, k * STEPS + ((c - 1) * SPC if c > 0 else -LS))
                    if isinstance(k, int) and k == 0 and c == 1:
                        dve.wait_ge(last_chunk_ordered, 1)
                    src = packed_in[:, par, c * w:(c + 1) * w]
                    n = steps_of(c)
                else:
                    dve.wait_ge(weights_made, k * STEPS + (c - 1) * SPC)
                    src = packed_in[:, par, bass.ds(c * w, w)]
                    n = SPC
                nc.vector.tensor_tensor(unpacked[:, slot, 0:n, 0:w], src.bitcast(U32)[:, None, :].to_broadcast([P, n, w]),
                                        bit_of[:, 0:n, None].to_broadcast([P, n, w]), ALU.bitwise_and).then_inc(mask_unpacked, 1)

            def layer2(k, par, width, first):
                if first:
                    unpack(0, 0, IB, 0, 0)
                    right_factor(0)
                    dve.wait_ge(f_ready, 1)
                    dve.wait_ge(x1_stored_dram, 16 * (NB + 1))
                    dve.wait_ge(x1_kept, NB + 1)
                    dve.wait_ge(scores_product, NB + 1)
                else:
                    dve.wait_ge(f_ready, 2)

                def chunk(c, slot):
                    dve.wait_ge(mask_unpacked, k * NC + c + 1)
                    for n in range(steps_of(c) if isinstance(c, int) else SPC):
                        b = c * SPC + n
                        if first and b % 3 == 0 and b > 0:
                            right_factor(b // 3)
                        if not isinstance(c, int) or c > 0:
                            dve.wait_ge(step_contracted, k * STEPS + b - SPC + 1)
                        elif not first:
                            dve.wait_ge(step_contracted, k * STEPS + (n - LS + 1 if n < LS else n - LS - SPC + 1))
                        if isinstance(c, int):
                            scalar = c_col[:, b:b + 1]
                        else:
                            scalar = c_col[:, bass.ds(c * SPC + n, 1)]
                        weights(k, par, width, scalar, unpacked[:, slot, n, 0:width // 4].bitcast(U8), n)
                        if n == 2:
                            if not isinstance(c, int) or c < NC - 1:
                                unpack(k, par, width, c + 1, 1 - slot)
                            elif not (isinstance(k, int) and k == NB):
                                unpack(k + 1, 1 - par, IB, 0, 0)

                if first:
                    for c in range(NC):
                        chunk(c, c % 2)
                    return
                chunk(0, 0)
                denominators(k - 1, IB)
                with dve.Fori(1, NC - 2, 2) as c:
                    chunk(c, 1)
                    chunk(c + 1, 0)
                row_stats(k - 1, IB)
                chunk(NC - 1, 1)
                scaled(k - 1, IB)

            blocks(dve, layer2)
            denominators(NB, TW)
            epilogue(dve, nc.vector, NB, TW, False)
            row_stats(NB, TW)
            scaled(NB, TW)

        @block.scalar
        def _(act):
            for c in range(NC):
                n = min(N, (c + 1) * JC) - c * JC
                act.wait_ge(item_turned, c + 1)
                if c >= 2:
                    act.wait_ge(h_product, c - 1)
                for q in range(-(-n // IB)):
                    src = item_banks[c % 2][q][:, 0:min(IB, n - q * IB)]
                    if c < NC - 1:
                        to = item_t[:, c % 2, :].rearrange("p (s a j) -> p a s j", a=A, j=Q)[:, 2 * q:2 * q + 2, :, :]
                        last = nc.scalar.copy(to, src.rearrange("p (a s j) -> p a s j", a=A // 2, j=Q))
                    else:
                        if q == 0:
                            act.wait_ge(constants_made, 6)
                        nc.scalar.copy(item_plain[:, q * IB:min(n, (q + 1) * IB)], src).then_inc(item_plain_made, 1)
                if c == NC - 1:
                    act.wait_ge(item_plain_made, 2)
                    last = in_step_order(nc.scalar.copy, item_t[:, c % 2, :], item_plain, True)[-1]
                last.then_inc(item_turned_sb, 1)

            def mask_chunk(k, c, width):
                act.wait_ge(half_turned, k * (2 * NC) + 2 * c + 2)
                if not (isinstance(k, int) and k * NC + c < 2):
                    act.wait_ge(packed_to_4, k * NC + c - 1)
                w = steps_of(c) * width
                nc.scalar.activation(mask_out[:, c % 2, 0:w], adj_t[:, c % 2, 0:w], ACT.Sign).then_inc(mask_made, 1)

            def store_masks(k, half, width):
                act.wait_ge(packed_to_1, k * NC + (half + 1) * HC)
                lo, hi = half * HC * width, (half + 1) * HC * width
                act.dma_start(mask_dram[bass.ds(k, 1), :, lo:hi].rearrange("o p w -> (o p) w").bitcast(U32),
                              packed[:, half, 0:HC * width // 4]).then_inc(masks_stored[half], 16)

            def relu(k, par, width):
                act.wait_ge(chunk_contracted, NC * (k + 1))
                if not (isinstance(k, int) and k == 0):
                    act.wait_ge(z_rows_ready, k)
                nc.scalar.activation(yz[:, 0:width], acc[par][:, 0:width], ACT.Relu, bias=b_user_col[:, 0:1]).then_inc(relu_done, 1)

            def x_copied(k, width, live):
                act.wait_ge(x_turned, k + 1)
                if not (isinstance(k, int) and k == 0):
                    act.wait_ge(residual_added, k)
                nc.scalar.copy(x_t[:, 0:live], ps_x[:, 0:live]).then_inc(x_turned_sb, 1)

            def deviations(k, width):
                nt = len(tiles_of(width))
                act.wait_ge(norm1_moments, k + 1)
                if not (isinstance(k, int) and k == 0):
                    act.wait_ge(norm1_reciprocals, k)
                nc.scalar.activation(std_o[:, 0:nt], mv[:, 0:nt, 1:2].rearrange("p t o -> p (t o)"), ACT.Sqrt,
                                     bias=eps_col[:, 0:1]).then_inc(norm1_deviations, 1)

            def x1_stored(k):
                act.wait_ge(x1_rows_ready, k + 1)
                act.dma_start(x1_dram[bass.ds(k * IB, IB), :].rearrange("(t p) d -> p t d", p=P), x1_rows[:, :, :]).then_inc(x1_stored_dram, 16)

            def x1_copied(k, width):
                act.wait_ge(x1_turned, k + 1)
                if not (isinstance(k, int) and k == 0):
                    act.wait_ge(x1_kept, k)
                    act.wait_ge(scores_product, k)
                    act.wait_ge(x1_summed, k)
                nc.scalar.copy(x1_blk[:, 0:width], ps_back[:, 0:width]).then_inc(x1_turned_sb, 1)

            def scores_out(k, width):
                act.wait_ge(scores_product, k + 1)
                if not (isinstance(k, int) and k == 0):
                    act.wait_ge(s_stored_dram, 16 * k)
                    act.wait_ge(t_max_taken, k)
                for t, m in tiles_of(width):
                    if t == 0 or m < P:
                        n = width // P if t == 0 else 1
                        last = nc.scalar.copy(ts_col[0:m, t:t + n, :], ps_ts[0:m, 2 * t:2 * t + 2 * n].rearrange("p (t o) -> p t o", o=2))
                last.then_inc(scores_sb, 1)
                act.wait_ge(scores_sb, k + 1)
                with nc.allow_non_contiguous_dma(reason="one word for each row of the block"):
                    act.dma_start(s_dram[:, bass.ds(k * IB, IB)].rearrange("o (t p w) -> p (o t) w", p=P, w=1), ts_col[:, :, 1:2]).then_inc(s_stored_dram, 16)

            def layer1(k, par, width, first):
                live = width if width == IB else TAIL
                if first:
                    x_copied(k, width, live)
                for c in range(NC):
                    mask_chunk(k, c, width)
                    if not first:
                        if c == 0:
                            relu(k - 1, 1 - par, IB)
                        if c == 1:
                            store_masks(k - 1, 1, IB)
                        if c == at(3):
                            x_copied(k, width, live)
                            deviations(k - 1, IB)
                        if c == at(4):
                            x1_stored(k - 1)
                        if c == at(5):
                            x1_copied(k - 1, IB)
                        if c == at(7):
                            scores_out(k - 1, IB)
                    if c == HC + 1:
                        store_masks(k, 0, width)

            blocks(act, layer1)

            def wh_copied(lo, hi):
                for g in range(lo, min(hi, WHG)):
                    n = min(STEPS, 3 * g + 3) - 3 * g
                    act.wait_ge(wh_product, g + 1)
                    nc.scalar.copy(area_h[:, 3 * g * DEN:(3 * g + n) * DEN], wh_bank(g)[:, 0:n * DEN]).then_inc(wh_sb, 1)

            def columns(lo, hi):
                t = awh[:, lo:hi, D:DEN]
                nc.scalar.activation(a_col[:, lo:hi, None], t, ACT.Exp, bias=shift[:, 0:1]).then_inc(columns_made, 1)
                nc.scalar.activation(c_col[:, lo:hi, None], t, ACT.Exp, bias=shift[:, 1:2], scale=-(1.0 - SLOPE)).then_inc(columns_made, 1)

            def f_part(i, lo, hi):
                act.wait_ge(s_capped[i], 1)
                nc.scalar.activation(f_row[:, lo:hi], f_row[:, lo:hi], ACT.Exp, bias=shift[:, 1:2], scale=1.0 - SLOPE).then_inc(f_ready, 1)

            relu(NB, 1, TW)
            wh_copied(0, min(3, WHA))
            deviations(NB, TW)
            wh_copied(3, min(5, WHA))
            x1_copied(NB, TW)
            x1_stored(NB)
            wh_copied(5, min(7, WHA))
            scores_out(NB, TW)
            nc.scalar.activation(table_warm[:, :], eps_col[:, :], ACT.Exp)
            wh_copied(7, WHA)
            store_masks(NB, 1, TW)

            act.wait_ge(shifts_made, 1)
            act.wait_ge(wh_sb, WHA)
            columns(0, 3 * WHA)
            f_part(0, 0, IB)
            for g in range(WHA, WHG):
                wh_copied(g, g + 1)
                act.wait_ge(wh_sb, g + 1)
                columns(3 * g, min(STEPS, 3 * g + 3))
            f_part(1, IB, NP)
            act.wait_ge(wh_mean_product, 1)
            nc.scalar.copy(wh_mean[:, :], banks[4][:, 0:D]).then_inc(wh_mean_ready, 1)

            def copied_out(k, par, width):
                act.wait_ge(step_contracted, STEPS * (k + 1))
                if not (isinstance(k, int) and k == 0):
                    act.wait_ge(quotient_steps, 3 * k)
                for q in range(2):
                    m = min(2, len(tiles_of(width)) - 2 * q)
                    nc.scalar.copy(o_sb[:, 2 * q:2 * q + m, :],
                                   banks[2 * par + q][:, 0:m * DEN].rearrange("p (t d) -> p t d", d=DEN)).then_inc(sums_sb, 1)

            def elu_exp(k, width):
                w = len(tiles_of(width)) * D
                act.wait_ge(elu_halves, 2 * k + 2)
                nc.scalar.activation(el[:, 1, 0:w], el[:, 1, 0:w], ACT.Exp).then_inc(elu_exp_done, 1)

            def stored(k, width):
                nt = len(tiles_of(width))
                act.wait_ge(norm2_moments, k + 1)
                if not (isinstance(k, int) and k == 0):
                    act.wait_ge(rows_ready, k)
                nc.scalar.activation(std_o[:, 0:nt], mv[:, 0:nt, 1:2].rearrange("p t o -> p (t o)"), ACT.Sqrt,
                                     bias=eps_col[:, 0:1]).then_inc(norm2_deviations, 1)
                act.wait_ge(rows_ready, k + 1)
                if width == IB:
                    rows = out[bass.ds(k * IB, IB), :].rearrange("(t p) d -> p t d", p=P)
                    for t in (0, TPB // 2):
                        act.dma_start(rows[:, t:t + TPB // 2, :], o_out[:, t:t + TPB // 2, :]).then_inc(rows_stored, 16)
                else:
                    full = TAIL // P
                    act.dma_start(out[NB * IB:NB * IB + full * P, :].rearrange("(t p) d -> p t d", p=P), o_out[:, 0:full, :]).then_inc(rows_stored, 16)
                    act.dma_start(out[NB * IB + full * P:N, :], o_out[0:TAIL - full * P, full, :]).then_inc(rows_stored, 16)

            def layer2(k, par, width, first):
                copied_out(k, par, width)
                elu_exp(k, width)
                stored(k, width)

            blocks(act, layer2)
            act.wait_ge(rows_stored, 32 * (NB + 1))


_INS = ['x', 'adj', 'L0_gnn_item_feat', 'L0_gnn_W_item', 'L0_gnn_b_item', 'L0_gnn_W_user', 'L0_gnn_b_user', 'L1_gnn_W', 'L1_gnn_a']


def kernel(**inputs):
    import numpy as _np
    import concourse.bacc as _bacc
    from concourse import mybir as _mybir
    from concourse.bass_utils import run_bass_kernel_spmd as _run

    nc = _bacc.Bacc("TRN2", target_bir_lowering=False, num_devices=1)
    arrays, args = {}, []
    for name in _INS:
        a = _np.ascontiguousarray(inputs[name])
        arrays[f"in_{name}_dram"] = a
        args.append(nc.dram_tensor(f"in_{name}_dram", a.shape, _mybir.dt.from_np(a.dtype), kind="ExternalInput").ap())
    out = nc.dram_tensor("out_0_dram", inputs['x'].shape, _mybir.dt.float32, kind="ExternalOutput").ap()
    resnorm_two_graph_layers(nc, *args, out)
    r = _run(nc, [arrays], core_ids=[0])
    return r.results[0]["out_0_dram"]
```
